# Optimizing a Trainium2 kernel written in Bass

```python
import numpy as np
import jax
import jax.numpy as jnp

def _softmax(x, axis=-1):
    return jax.nn.softmax(x, axis=axis)

def _gelu(x):
    return jax.nn.gelu(x, approximate=True)

def _silu(x):
    return jax.nn.silu(x)

def _sigmoid(x):
    return jax.nn.sigmoid(x)

def _layernorm(x, axis=-1, eps=1e-05):
    m = jnp.mean(x, axis=axis, keepdims=True)
    v = jnp.var(x, axis=axis, keepdims=True)
    return (x - m) / jnp.sqrt(v + eps)

def _scatter_add(tgt, idx, src, axis=0):
    return tgt.at[idx].add(src)

def _segment_sum(src, seg, n):
    return jax.ops.segment_sum(src, seg, n)
kernel_name = 'mk_gnn_resnorm_d2_gnn_r8_275127'

def setup_inputs(seed: int=0):
    np.random.seed(seed)
    _w = jnp.asarray

    def _rec_inputs():
        import jax
        import jax.numpy as jnp
        _gk = jax.random.key(seed)
        x = -0.0005121 + 1.001 * jax.random.normal(jax.random.fold_in(_gk, 1), (12500, 32), jnp.float32)
        src = jax.random.randint(jax.random.fold_in(_gk, 2), (200000,), 0, 12500, jnp.int32)
        dst = jnp.minimum((12500 * jax.random.uniform(jax.random.fold_in(_gk, 3), (200000,)) ** 2.0).astype(jnp.int32), 99999)
        _o = jnp.argsort(dst, stable=True)
        src = src[_o]
        dst = dst[_o]
        edge_attr3_2x32 = -8.16379e-05 + 0.999858 * jax.random.normal(jax.random.fold_in(_gk, 12), (200000, 2, 32), jnp.float32)
        return (x, src, dst, edge_attr3_2x32)
    x, src, dst, edge_attr3_2x32 = _rec_inputs()

    def _L0_gnn_setup():
        import jax, jax.numpy as jnp
        import numpy as np
        N_NODES = 12500
        N_EDGES = 200000
        D_IN, D_HID, D_OUT = (32, 64, 32)

        def sage_conv(x, edge_index, W_l, b_l, W_r, num_segments):
            src, dst = (edge_index[0], edge_index[1])
            agg = jax.ops.segment_sum(x[src], dst, num_segments=num_segments)
            return agg @ W_l.T + b_l + x @ W_r.T
        key = jax.random.key(seed)
        ks = jax.random.split(key, 8)
        x = jax.random.normal(ks[0], (N_NODES, D_IN), dtype=jnp.float32)
        edge_index = jax.random.randint(ks[1], (2, N_EDGES), 0, N_NODES, dtype=jnp.int64)
        s_in = 1.0 / np.sqrt(D_IN)
        s_hid = 1.0 / np.sqrt(D_HID)
        W_l_in = jax.random.normal(ks[2], (D_HID, D_IN), dtype=jnp.float32) * s_in
        b_l_in = jnp.zeros((D_HID,), dtype=jnp.float32)
        W_r_in = jax.random.normal(ks[3], (D_HID, D_IN), dtype=jnp.float32) * s_in
        W_l_out = jax.random.normal(ks[4], (D_OUT, D_HID), dtype=jnp.float32) * s_hid
        b_l_out = jnp.zeros((D_OUT,), dtype=jnp.float32)
        W_r_out = jax.random.normal(ks[5], (D_OUT, D_HID), dtype=jnp.float32) * s_hid
        return {'x': x, 'edge_index': edge_index, 'W_l_in': W_l_in, 'b_l_in': b_l_in, 'W_r_in': W_r_in, 'W_l_out': W_l_out, 'b_l_out': b_l_out, 'W_r_out': W_r_out}
    _L0_gnn_all = _L0_gnn_setup()
    _L0_gnn_in = {k: v for k, v in _L0_gnn_all.items() if k in ('W_l_in', 'b_l_in', 'W_r_in', 'W_l_out', 'b_l_out', 'W_r_out')}
    del _L0_gnn_all

    def _L1_gnn_setup():
        import jax, jax.numpy as jnp
        import numpy as np
        N = 6250
        E = 200000
        H = 2
        F = 32
        IN = 32
        OUT = 32
        NEG_SLOPE = 0.2
        key = jax.random.key(seed)
        ks = jax.random.split(key, 11)
        s = 0.1
        return {'feat': jax.random.normal(ks[0], (N, IN), jnp.float32), 'r_feat': jax.random.normal(ks[1], (E, H, F), jnp.float32), 'src': jax.random.randint(ks[2], (E,), 0, N), 'dst': jax.random.randint(ks[3], (E,), 0, N), 'W1': jax.random.normal(ks[4], (IN, OUT), jnp.float32) * s, 'b1': jnp.zeros((OUT,), jnp.float32), 'W2s': jax.random.normal(ks[5], (IN, H * F), jnp.float32) * s, 'b2s': jnp.zeros((H * F,), jnp.float32), 'W2d': jax.random.normal(ks[6], (IN, H * F), jnp.float32) * s, 'b2d': jnp.zeros((H * F,), jnp.float32), 'attn': jax.random.normal(ks[7], (1, H, F), jnp.float32) * s}
    _L1_gnn_all = _L1_gnn_setup()
    _L1_gnn_in = {k: v for k, v in _L1_gnn_all.items() if k in ('W1', 'b1', 'W2s', 'b2s', 'W2d', 'b2d', 'attn')}
    del _L1_gnn_all
    return {'x': x, 'src': src, 'dst': dst, 'edge_attr3_2x32': edge_attr3_2x32, 'L0_gnn_W_l_in': _L0_gnn_in['W_l_in'], 'L0_gnn_b_l_in': _L0_gnn_in['b_l_in'], 'L0_gnn_W_r_in': _L0_gnn_in['W_r_in'], 'L0_gnn_W_l_out': _L0_gnn_in['W_l_out'], 'L0_gnn_b_l_out': _L0_gnn_in['b_l_out'], 'L0_gnn_W_r_out': _L0_gnn_in['W_r_out'], 'L1_gnn_W1': _L1_gnn_in['W1'], 'L1_gnn_b1': _L1_gnn_in['b1'], 'L1_gnn_W2s': _L1_gnn_in['W2s'], 'L1_gnn_b2s': _L1_gnn_in['b2s'], 'L1_gnn_W2d': _L1_gnn_in['W2d'], 'L1_gnn_b2d': _L1_gnn_in['b2d'], 'L1_gnn_attn': _L1_gnn_in['attn']}

def reference(x, src, dst, edge_attr3_2x32, L0_gnn_W_l_in, L0_gnn_b_l_in, L0_gnn_W_r_in, L0_gnn_W_l_out, L0_gnn_b_l_out, L0_gnn_W_r_out, L1_gnn_W1, L1_gnn_b1, L1_gnn_W2s, L1_gnn_b2s, L1_gnn_W2d, L1_gnn_b2d, L1_gnn_attn):
    import jax
    import jax.numpy as jnp

    def _L0_gnn_ref(x, edge_index, W_l_in, b_l_in, W_r_in, W_l_out, b_l_out, W_r_out):
        import jax, jax.numpy as jnp
        import numpy as np
        N_NODES = 12500
        N_EDGES = 200000
        D_IN, D_HID, D_OUT = (32, 64, 32)

        def sage_conv(x, edge_index, W_l, b_l, W_r, num_segments):
            src, dst = (edge_index[0], edge_index[1])
            agg = jax.ops.segment_sum(x[src], dst, num_segments=num_segments)
            return agg @ W_l.T + b_l + x @ W_r.T
        n = x.shape[0]
        h = sage_conv(x, edge_index, W_l_in, b_l_in, W_r_in, n)
        h = jax.nn.relu(h)
        out = sage_conv(h, edge_index, W_l_out, b_l_out, W_r_out, n)
        return out

    def _L1_gnn_ref(feat, r_feat, src, dst, W1, b1, W2s, b2s, W2d, b2d, attn):
        import jax, jax.numpy as jnp
        import numpy as np
        N = 6250
        E = 200000
        H = 2
        F = 32
        IN = 32
        OUT = 32
        NEG_SLOPE = 0.2
        n = feat.shape[0]
        feat_src = (feat @ W2s + b2s).reshape(n, H, F)
        feat_dst = (feat @ W2d + b2d).reshape(n, H, F)
        en = feat_src[src]
        ev = feat_dst[dst]
        e = jax.nn.leaky_relu(en + ev, negative_slope=NEG_SLOPE)
        e = jnp.sum(e * attn, axis=-1, keepdims=True)
        m = jax.ops.segment_max(e, dst, num_segments=n)
        m = jnp.where(jnp.isfinite(m), m, 0.0)
        ee = jnp.exp(e - m[dst])
        denom = jax.ops.segment_sum(ee, dst, num_segments=n)
        alpha = ee / jnp.maximum(denom[dst], 1e-09)
        msg = jax.nn.softmax(en * r_feat * alpha, axis=-1)
        g_agg = jax.ops.segment_sum(msg, dst, num_segments=n)
        g_sum = jnp.sum(g_agg, axis=1)
        rst = (feat + g_sum) @ W1 + b1
        return rst
    edge_index = jnp.stack([src, dst])
    x = _layernorm(x + _L0_gnn_ref(x, edge_index, L0_gnn_W_l_in, L0_gnn_b_l_in, L0_gnn_W_r_in, L0_gnn_W_l_out, L0_gnn_b_l_out, L0_gnn_W_r_out), axis=-1)
    x = _layernorm(x + _L1_gnn_ref(x, edge_attr3_2x32, src, dst, L1_gnn_W1, L1_gnn_b1, L1_gnn_W2s, L1_gnn_b2s, L1_gnn_W2d, L1_gnn_b2d, L1_gnn_attn), axis=-1)
    return x

_drawn_inputs = setup_inputs


def setup_inputs(seed=0):
    import zlib

    import numpy as np

    out = dict(_drawn_inputs(seed))
    spreads = {'L0_gnn_b_l_in': (0.0, 0.296),
     'L0_gnn_b_l_out': (0.0, 0.8),
     'L1_gnn_b1': (0.0, 0.1),
     'L1_gnn_b2s': (0.0, 0.8),
     'L1_gnn_b2d': (0.0, 0.8)}
    factors = {'edge_attr3_2x32': 8.0, 'L1_gnn_W2s': 8.0, 'L1_gnn_W2d': 8.0, 'L1_gnn_attn': 8.0}
    for name, (base, spread) in spreads.items():
        noise = np.random.default_rng([zlib.crc32(name.encode()), seed]).standard_normal(out[name].shape)
        drawn = base * np.exp(spread * noise) if base else spread * noise
        out[name] = jnp.asarray(drawn.astype(out[name].dtype))
    for name, factor in factors.items():
        out[name] = (out[name] * factor).astype(out[name].dtype)
    return out
```

```python
import concourse.bass as bass
from concourse import mybir
from concourse.alu_op_type import AluOpType as ALU
from contextlib import ExitStack

F32 = mybir.dt.float32
I32 = mybir.dt.int32
ACT = mybir.ActivationFunctionType
AX = mybir.AxisListType
DVE_ENGINE = [mybir.EngineType.DVE]
SP_ENGINE = [mybir.EngineType.SP]

P = 128
HEAD = 4
K = 4
GROUP = P * K
WINDOW = 128
SLOTS = 4
SG = 2
ST = SG * K
IG = SLOTS * SG
F = 32
HID = 64
H = 2
BIG = 1.0e38
EPS = 1e-5
SLOPE = 0.2
CLAMPED = "set-up clamps the starts"
NOWHERE = 1 << 20


def sizes(n_nodes, n_edges):
    iters = -(-n_edges // (GROUP * IG))
    groups = iters * IG
    rows = groups // K
    chunks = -(-(n_nodes + WINDOW) // GROUP)
    return iters, groups, rows, chunks


def iterations(engine, count, body):
    body(0, True)
    with engine.Fori(1, count) as it:
        body(it, False)


class Link:

    def __init__(self, engine, sem):
        self.engine, self.sem, self.count, self.base = engine, sem, 0, 0

    def __call__(self, instruction):
        instruction.then_inc(self.sem, 1)
        self.count += 1
        self.engine.wait_ge(self.sem, self.base + self.count)

    def iteration(self, i, per_iteration, before):
        self.base, self.count = i * per_iteration + before, 0

    def after(self, total):
        self.base, self.count = 0, total


def wide(ap, at, shape):
    return ap.unsqueeze(at).to_broadcast(shape)


def build(nc, x, src, dst, edge_attr, wl_in, bl_in, wr_in, wl_out, bl_out, wr_out,
          w1, b1, w2s, b2s, w2d, b2d, attn, out):
    N, E = x.shape[0], src.shape[0]
    IT, G, J, NCH = sizes(N, E)
    LONG = K * GROUP
    NK = NCH * K
    FULLJ, RESTJ = E // LONG, E % LONG
    assert J <= P and RESTJ % K == 0 and N % K == 0

    y_dram = nc.dram_tensor("y_scratch", (NCH * GROUP, F), F32, kind="Internal").ap()
    fs_dram = nc.dram_tensor("fs_scratch", (NCH * GROUP, HID), F32, kind="Internal").ap()
    fd_dram = nc.dram_tensor("fd_scratch", (NCH * GROUP, HID), F32, kind="Internal").ap()
    en_dram = nc.dram_tensor("en_scratch", (IT * SLOTS, P, ST * HID), F32, kind="Internal").ap()

    def skewed(engine, chunks, lags, step, unroll=2, peel=0):
        loops = (chunks - HEAD - peel) // unroll
        for c in range(HEAD):
            step(c, c % unroll, c, c)
        with engine.Fori(0, loops) as i:
            for u in range(unroll):
                step(i * unroll + (HEAD + u), u, HEAD, chunks - 1)
        for c in range(HEAD + unroll * loops, chunks + lags):
            step(c, c % unroll, c, c)

    def inside(chunks, lo, hi, lag):
        return lo - lag >= 0 and hi - lag < chunks

    with ExitStack() as whole:
        def sb(name, shape, dt=F32, ctx=whole):
            return ctx.enter_context(nc.sbuf_tensor(name, shape, dt))

        ident = sb("ident", [P, P])
        iota = sb("iota", [P, WINDOW])
        ones = sb("ones", [1, P])
        attn_sb = sb("attn_sb", [P, HID])
        wl_in_t = sb("wl_in_t", [F, P])
        wr_in_t = sb("wr_in_t", [F, P])
        b_in = sb("b_in", [HID, 1])
        w_out_t = sb("w_out_t", [HID, HID])
        w_node = sb("w_node", [F + 1, 2 * HID + F])
        w1_twice = sb("w1_twice", [HID, F])
        table_a = sb("table_a", [P, NCH * GROUP])
        scratch = sb("scratch", [P, 16400])
        nodes = sb("nodes", [P, NCH, K, F])
        rest = sb("rest", [P, NCH, K, F])
        src_idx = sb("src_idx", [P, G + SG, K], I32)
        dst_rel = sb("dst_rel", [P, G + SG, K])
        e_tab = sb("e_tab", [P, G, K, H])
        win = sb("win", [1, G], I32)
        gath = sb("gath", [P, SLOTS, ST, HID])
        idx_buf = sb("idx_buf", [P, SLOTS, ST], I32)
        onehot = sb("onehot", [P, 2, ST, WINDOW])
        flat_nodes = nodes[:, :, :, :].rearrange("p c k f -> p (c k) f")
        table_b = scratch[:, 0:NCH * GROUP]

        with ExitStack() as ctx:
            rows_i = scratch[:, 0:LONG].bitcast(I32)
            rows_f = scratch[:, LONG:3 * LONG].rearrange("p (w q) -> p w q", w=2)
            iota_i = sb("iota_i", [P, P], I32, ctx)
            pid_i = sb("pid_i", [P, 1], I32, ctx)
            pid = sb("pid", [P, 1], F32, ctx)
            dst_col = sb("dst_col", [P, G, K], F32, ctx)
            win_f = sb("win_f", [1, G], F32, ctx)
            bl_out_b = sb("bl_out_b", [P, F], F32, ctx)
            w_rows = sb("w_rows", [HID, 4, HID], F32, ctx)
            ps_t = ctx.enter_context(nc.psum_tensor("ps_t", [P, 16, P], F32))
            ps_w = ctx.enter_context(nc.psum_tensor("ps_w", [P, 4, P], F32))
            ps_b = ctx.enter_context(nc.psum_tensor("ps_b", [P, 512], F32))
            pads_set = ctx.enter_context(nc.semaphore("pads_set"))
            src_loaded = ctx.enter_context(nc.semaphore("src_loaded"))
            dst_loaded = ctx.enter_context(nc.semaphore("dst_loaded"))
            x_loaded = ctx.enter_context(nc.semaphore("x_loaded"))
            w_loaded = ctx.enter_context(nc.semaphore("w_loaded"))
            iotas = ctx.enter_context(nc.semaphore("iotas"))
            consts = ctx.enter_context(nc.semaphore("consts"))
            src_used = ctx.enter_context(nc.semaphore("src_used"))
            link_sem = ctx.enter_context(nc.semaphore("setup_link"))
            rows_ready = ctx.enter_context(nc.semaphore("rows_ready"))
            turned = ctx.enter_context(nc.semaphore("turned"))
            turned_used = ctx.enter_context(nc.semaphore("turned_used"))
            w_turned = ctx.enter_context(nc.semaphore("w_turned"))
            win_ready = ctx.enter_context(nc.semaphore("win_ready"))
            win_spread = ctx.enter_context(nc.semaphore("win_spread"))
            block = ctx.enter_context(nc.Block())

            @block.gpsimd
            def _(pool):
                pool.iota(iota_i[:, :], [[1, P]], base=0, channel_multiplier=0).then_inc(iotas, 1)
                pool.iota(pid_i[:, :], [[0, 1]], base=0, channel_multiplier=1).then_inc(iotas, 1)
                pool.memset(nodes[:, N // GROUP:NCH, :, :], 0.0).then_inc(pads_set, 1)
                pool.memset(w_node[:, :], 0.0).then_inc(pads_set, 1)

            @block.sync
            def _(sp):
                sp.wait_ge(consts, 1)
                sp.dma_start(rows_i[0:FULLJ, :], src[0:FULLJ * LONG].rearrange("(j q) -> j q", q=LONG))\
                  .then_inc(src_loaded, 16)
                sp.dma_start(rows_i[FULLJ:FULLJ + 1, 0:RESTJ],
                             src[FULLJ * LONG:E].rearrange("(j q) -> j q", q=RESTJ)).then_inc(src_loaded, 16)
                sp.wait_ge(pads_set, 2)
                full = N // GROUP
                sp.dma_start(nodes[:, 0:full, :, :].rearrange("p c k f -> p c (k f)"),
                             x[0:full * GROUP, :].rearrange("(c p k) f -> p c (k f)", p=P, k=K)).then_inc(x_loaded, 16)
                left = (N - full * GROUP) // K
                sp.dma_start(nodes[0:left, full, :, :].rearrange("p k f -> p (k f)"),
                             x[full * GROUP:N, :].rearrange("(p k) f -> p (k f)", k=K)).then_inc(x_loaded, 16)
                sp.wait_ge(consts, 3)
                sp.dma_start(rows_i[0:FULLJ, :], dst[0:FULLJ * LONG].rearrange("(j q) -> j q", q=LONG))\
                  .then_inc(dst_loaded, 16)
                sp.dma_start(rows_i[FULLJ:FULLJ + 1, 0:RESTJ],
                             dst[FULLJ * LONG:E].rearrange("(j q) -> j q", q=RESTJ)).then_inc(dst_loaded, 16)
                sp.wait_ge(src_loaded, 32)
                sp.wait_ge(dst_loaded, 32)
                sp.wait_ge(x_loaded, 32)

            @block.scalar
            def _(act):
                act.dma_start(w_rows[0:HID, 0, 0:F], wl_in).then_inc(w_loaded, 16)
                act.dma_start(w_rows[0:HID, 1, 0:F], wr_in).then_inc(w_loaded, 16)
                act.dma_start(w_rows[0:F, 2, :], wl_out).then_inc(w_loaded, 16)
                act.dma_start(w_rows[0:F, 3, :], wr_out).then_inc(w_loaded, 16)
                act.dma_start(b_in[:, :], bl_in.rearrange("(f a) -> f a", a=1)).then_inc(w_loaded, 16)
                act.dma_start(bl_out_b[:, :], bl_out.rearrange("(a f) -> a f", a=1).to_broadcast([P, F])).then_inc(w_loaded, 16)
                act.dma_start(attn_sb[:, :], attn.rearrange("a h f -> a (h f)").to_broadcast([P, HID])).then_inc(w_loaded, 16)
                act.wait_ge(pads_set, 2)
                act.dma_start(w_node[0:F, 0:HID], w2s).then_inc(w_loaded, 16)
                act.dma_start(w_node[0:F, HID:2 * HID], w2d).then_inc(w_loaded, 16)
                act.dma_start(w_node[0:F, 2 * HID:2 * HID + F], w1).then_inc(w_loaded, 16)
                act.dma_start(w_node[F:F + 1, 0:HID], b2s.rearrange("(a f) -> a f", a=1)).then_inc(w_loaded, 16)
                act.dma_start(w_node[F:F + 1, HID:2 * HID], b2d.rearrange("(a f) -> a f", a=1)).then_inc(w_loaded, 16)
                act.dma_start(w_node[F:F + 1, 2 * HID:2 * HID + F], b1.rearrange("(a f) -> a f", a=1)).then_inc(w_loaded, 16)
                act.dma_start(w1_twice[0:F, :], w1).then_inc(w_loaded, 16)
                act.dma_start(w1_twice[F:HID, :], w1).then_inc(w_loaded, 16)
                act.wait_ge(w_loaded, 15 * 16)

            @block.vector
            def _(dve):
                link = Link(dve, link_sem)
                last = min(96, FULLJ // 32 * 32)
                link(dve.memset(rows_i[last:P, :], 0))
                dve.memset(ones[:, :], 1.0).then_inc(consts, 1)
                dve.wait_ge(iotas, 2)
                dve.tensor_copy(iota[:, :], iota_i[:, 0:WINDOW])
                link(dve.tensor_copy(pid[:, :], pid_i[:, :]))
                dve.memset(table_a[:, :], 0.0)
                dve.memset(wl_in_t[:, :], 0.0)
                dve.memset(wr_in_t[:, :], 0.0)
                link(dve.tensor_scalar(ident[:, :], iota_i[:, :], pid[:, 0:1], None, ALU.is_equal))
                dve.wait_ge(src_loaded, 32)
                link(dve.tensor_copy(rows_f[0:J, 0, :], rows_i[0:J, :]))
                dve.memset(ones[:, :], 1.0).then_inc(consts, 1)
                link(dve.memset(rows_i[last:P, :], NOWHERE))
                dve.memset(ones[:, :], 1.0).then_inc(consts, 1)
                dve.wait_ge(dst_loaded, 32)
                link(dve.tensor_copy(rows_f[0:J, 1, :], rows_i[0:J, :]))
                dve.memset(ones[:, :], 1.0).then_inc(rows_ready, 1)
                dve.wait_ge(turned, 1)
                dve.tensor_copy(src_idx[:, 0:G, :].rearrange("p (j c) k -> p j (c k)", c=K),
                                ps_t[:, :, 0:J].rearrange("p a j -> p j a")).then_inc(turned_used, 1)
                dve.memset(src_idx[:, G:G + SG, :], 0)
                dve.wait_ge(turned, 2)
                link(dve.tensor_copy(dst_col[:, :, :].rearrange("p (j c) k -> p j (c k)", c=K),
                                     ps_t[:, :, 0:J].rearrange("p a j -> p j a")))
                link(dve.tensor_scalar(win_f[:, :], dst_col[0:1, :, 0], float(N), None, ALU.min))
                dve.tensor_copy(win[:, :], win_f[:, :]).then_inc(win_ready, 1)
                dve.wait_ge(win_spread, 1)
                dve.tensor_tensor(dst_rel[:, 0:G, :], dst_col[:, :, :],
                                  wide(ps_b[:, 0:G], 2, [P, G, K]), ALU.subtract)
                dve.memset(dst_rel[:, G:G + SG, :], float(NOWHERE))
                dve.wait_ge(w_turned, 1)
                dve.tensor_copy(wl_in_t[:, 0:HID], ps_w[0:F, 0, 0:HID])
                dve.tensor_copy(wr_in_t[:, 0:HID], ps_w[0:F, 1, 0:HID])
                dve.tensor_copy(w_out_t[:, 0:F], ps_w[0:HID, 2, 0:F])
                dve.tensor_copy(w_out_t[:, F:HID], ps_w[0:HID, 3, 0:F])

            @block.tensor
            def _(pe):
                pe.wait_ge(rows_ready, 1)
                for which in range(2):
                    if which:
                        pe.wait_ge(turned_used, 1)
                    for c in range(K):
                        for k in range(K):
                            t = pe.transpose(ps_t[:, c * K + k, 0:J],
                                             rows_f[0:J, which, c * GROUP + k:(c + 1) * GROUP:K], ident[0:J, 0:J])
                    t.then_inc(turned, 1)
                pe.wait_ge(w_loaded, 15 * 16)
                pe.transpose(ps_w[0:F, 0, 0:HID], w_rows[0:HID, 0, 0:F], ident[0:HID, 0:HID])
                pe.transpose(ps_w[0:F, 1, 0:HID], w_rows[0:HID, 1, 0:F], ident[0:HID, 0:HID])
                pe.transpose(ps_w[0:HID, 2, 0:F], w_rows[0:F, 2, :], ident[0:F, 0:F])
                pe.transpose(ps_w[0:HID, 3, 0:F], w_rows[0:F, 3, :], ident[0:F, 0:F]).then_inc(w_turned, 1)
                pe.wait_ge(win_ready, 1)
                pe.matmul(ps_b[:, 0:G], ones[0:1, :], win_f[0:1, :], start=True, stop=True).then_inc(win_spread, 1)

        def segment_sum_pass(tag, table_dram, table):
            with ExitStack() as ctx:
                ps = [ctx.enter_context(nc.psum_tensor(f"{tag}_ps{i}", [F, SG, WINDOW], F32)) for i in range(2)]
                sem = lambda n: ctx.enter_context(nc.semaphore(f"{tag}_{n}"))
                idx_staged = [sem(f"idx_staged{s}") for s in range(SLOTS)]
                gathered = [sem(f"gathered{s}") for s in range(SLOTS)]
                onehot_ready, opened = sem("onehot_ready"), sem("opened")
                summed = [sem(f"summed{s}") for s in range(SLOTS)]
                added = [sem(f"added{i}") for i in range(2)]
                block = ctx.enter_context(nc.Block())

                @block.scalar
                def _(act):
                    def iteration(it, first):
                        for s in range(SLOTS):
                            if not first:
                                act.wait_ge(gathered[s], it * (16 * ST))
                            act.activation(idx_buf[:, s, :],
                                           src_idx[:, bass.ds(it * IG + s * SG, SG), :].rearrange("p g k -> p (g k)"),
                                           ACT.Copy).then_inc(idx_staged[s], 1)
                    iterations(act, IT, iteration)

                @block.gpsimd
                def _(pool):
                    def iteration(it, first):
                        for s in range(SLOTS):
                            pool.wait_ge(idx_staged[s], it + 1)
                            if not first:
                                pool.wait_ge(summed[s], it)
                            pool.sem_inc(opened, 1)
                            for t in range(ST):
                                pool.indirect_dma_start(
                                    out=gath[:, s, t, 0:F], out_offset=None, in_=table_dram,
                                    in_offset=bass.IndirectOffsetOnAxis(ap=idx_buf[:, s, t:t + 1], axis=0),
                                ).then_inc(gathered[s], 16)
                    iterations(pool, IT, iteration)

                @block.tensor
                def _(pe):
                    def iteration(it, first):
                        for s in range(SLOTS):
                            par = s % 2
                            pe.wait_ge(onehot_ready, it * SLOTS + s + 1)
                            pe.wait_ge(gathered[s], it * (16 * ST) + 16 * ST)
                            if s >= 2 or not first:
                                pe.wait_ge(added[par], it * IG // 2 + s // 2 * SG)
                            for g in range(SG):
                                for k in range(K):
                                    m = pe.matmul(ps[par][:, g, :], gath[:, s, g * K + k, 0:F],
                                                  onehot[:, par, g * K + k, :], start=(k == 0), stop=(k == K - 1))
                            m.then_inc(summed[s], 1)
                    iterations(pe, IT, iteration)

                @block.vector
                def _(dve):
                    def make_onehot(par, first_group):
                        dve.tensor_tensor(
                            onehot[:, par, :, :], wide(iota[:, :], 1, [P, ST, WINDOW]),
                            wide(dst_rel[:, bass.ds(first_group, SG), :].rearrange("p g k -> p (g k)"), 2, [P, ST, WINDOW]),
                            ALU.is_equal).then_inc(onehot_ready, 1)

                    make_onehot(0, 0)
                    def iteration(it, first):
                        _, starts = nc.values_load_multi_w_load_instructions(
                            win[0:1, bass.ds(it * IG, IG)], engines=DVE_ENGINE, min_val=0, max_val=N,
                            skip_runtime_bounds_check_because=CLAMPED)
                        for s in range(SLOTS):
                            par = s % 2
                            if s or not first:
                                dve.wait_ge(summed[(s - 1) % SLOTS], it + (1 if s else 0))
                            make_onehot(1 - par, it * IG + (s + 1) * SG)
                            dve.wait_ge(summed[s], it + 1)
                            for g in range(SG):
                                if g or s:
                                    prev_par = par if g else 1 - par
                                    prev = s // 2 * SG + g if g else (s - 1) // 2 * SG + SG
                                    dve.wait_ge(added[prev_par], it * (IG // 2) + prev)
                                else:
                                    if not first:
                                        dve.wait_ge(added[1], it * (IG // 2))
                                at = table[0:F, bass.ds(starts[s * SG + g], WINDOW)]
                                dve.tensor_tensor(at, at, ps[par][:, g, :], ALU.add).then_inc(added[par], 1)
                    iterations(dve, IT, iteration)

        segment_sum_pass("sum_x", x, table_a)

        with ExitStack() as ctx:
            xt = sb("xt", [F, 2, K, P], F32, ctx)
            stage = sb("stage", [P, 2, K, F], F32, ctx)
            hid = sb("hid", [HID, 2, K, P], F32, ctx)
            y_sb = scratch[:, 0:NK * F].rearrange("p (c k f) -> p c k f", k=K, f=F)
            ps_x = [ctx.enter_context(nc.psum_tensor(f"ps_x{i}", [F, K, P], F32)) for i in range(2)]
            ps_h = [ctx.enter_context(nc.psum_tensor(f"ps_h{i}", [P, K, P], F32)) for i in range(2)]
            ps_y = [ctx.enter_context(nc.psum_tensor(f"ps_y{i}", [P, K, HID], F32)) for i in range(2)]
            sem = lambda n: ctx.enter_context(nc.semaphore(f"n0_{n}"))
            staged, x_turned, x_copied, h_summed, h_ready, y_summed, y_used, y_stored = map(
                sem, ("staged", "x_turned", "x_copied", "h_summed", "h_ready", "y_summed", "y_used", "y_stored"))
            block = ctx.enter_context(nc.Block())

            @block.tensor
            def _(pe):
                def step(c, par, lo, hi):
                    if inside(NCH, lo, hi, 0):
                        pe.wait_ge(staged, c + 1)
                        if lo >= 2:
                            pe.wait_ge(x_copied, c - 1)
                        for k in range(K):
                            t = pe.transpose(ps_x[par][:, k, :], stage[:, par, k, :], ident[:, :])
                        t.then_inc(x_turned, 1)
                    if inside(NCH, lo, hi, 1):
                        pe.wait_ge(x_copied, c)
                        if lo >= 3:
                            pe.wait_ge(h_ready, c - 2)
                        q = 1 - par
                        pe.matmul(ps_h[q][:, :, :], wl_in_t[:, :],
                                  table_a[0:F, bass.ds((c - 1) * GROUP, GROUP)].rearrange("f (p k) -> f k p", k=K),
                                  start=True, stop=False)
                        pe.matmul(ps_h[q][:, :, :], wr_in_t[:, :], xt[:, q, :, :], start=False, stop=True)\
                          .then_inc(h_summed, 1)
                    if inside(NCH, lo, hi, 2):
                        pe.wait_ge(h_ready, c - 1)
                        if lo >= 4:
                            pe.wait_ge(y_used, c - 3)
                        for k in range(K):
                            m = pe.matmul(ps_y[par][:, k, :], hid[:, par, k, :], w_out_t[:, :], start=True, stop=True)
                        m.then_inc(y_summed, 1)
                skewed(pe, NCH, 2, step)

            @block.scalar
            def _(act):
                def step(c, par, lo, hi):
                    if inside(NCH, lo, hi, 0):
                        act.wait_ge(x_turned, c + 1)
                        if lo >= 2:
                            act.wait_ge(h_summed, c - 1)
                        act.activation(xt[:, par, :, :], ps_x[par][:, :, :], ACT.Copy).then_inc(x_copied, 1)
                    if inside(NCH, lo, hi, 1):
                        act.wait_ge(h_summed, c)
                        if lo >= 3:
                            act.wait_ge(y_summed, c - 2)
                        act.activation(hid[:, 1 - par, :, :], ps_h[1 - par][0:HID, :, :], ACT.Relu, bias=b_in[:, 0:1])\
                           .then_inc(h_ready, 1)
                skewed(act, NCH, 1, step)

            @block.vector
            def _(dve):
                def step(c, par, lo, hi):
                    if inside(NCH, lo, hi, 0):
                        if lo >= 2:
                            dve.wait_ge(x_turned, c - 1)
                        dve.tensor_copy(stage[:, par, :, :], nodes[:, bass.ds(c, 1), :, :]
                                        .rearrange("p c k f -> p (c k) f")).then_inc(staged, 1)
                    if inside(NCH, lo, hi, 2):
                        dve.wait_ge(y_summed, c - 1)
                        dve.tensor_copy(y_sb[:, bass.ds(c - 2, 1), :, :].rearrange("p c k f -> p (c k) f"),
                                        ps_y[par][:, :, 0:F])
                        dve.tensor_copy(rest[:, bass.ds(c - 2, 1), :, :].rearrange("p c k f -> p (c k) f"),
                                        ps_y[par][:, :, F:HID]).then_inc(y_used, 1)
                skewed(dve, NCH, 2, step)

            @block.sync
            def _(sp):
                sp.wait_ge(y_used, NCH)
                sp.dma_start(y_dram.rearrange("(c p k) f -> p c (k f)", p=P, k=K),
                             y_sb.rearrange("p c k f -> p c (k f)")).then_inc(y_stored, 16)
                sp.wait_ge(y_stored, 16)

        with ExitStack() as ctx:
            block = ctx.enter_context(nc.Block())

            @block.vector
            def _(dve):
                dve.memset(table_b[0:F, :], 0.0)

            @block.gpsimd
            def _(pool):
                pool.memset(table_a[0:HID, :], 0.0)

        segment_sum_pass("sum_y", y_dram, table_b)

        def layer_norm(dve, act_sqrt, sqrt_done, link, v, work, mean, var, result):
            link(dve.tensor_reduce(mean[:, :], v, AX.X, ALU.add))
            link(dve.tensor_scalar(mean[:, :], mean[:, :], 1.0 / F, None, ALU.mult))
            link(dve.tensor_tensor(v, v, wide(mean[:, :], 2, [P, NK, F]), ALU.subtract))
            link(dve.tensor_tensor(work, v, v, ALU.mult))
            link(dve.tensor_reduce(var[:, :], work, AX.X, ALU.add))
            dve.tensor_scalar(var[:, :], var[:, :], 1.0 / F, EPS, ALU.mult, ALU.add).then_inc(act_sqrt, 1)
            dve.wait_ge(sqrt_done, 1)
            link(dve.reciprocal(var[:, :], var[:, :]))
            link(dve.tensor_tensor(result, v, wide(var[:, :], 2, [P, NK, F]), ALU.mult))

        with ExitStack() as ctx:
            mean = sb("mean", [P, NK], F32, ctx)
            var = sb("var", [P, NK], F32, ctx)
            xt = sb("x1t", [F + 1, 2, K, P], F32, ctx)
            stage = sb("stage1", [P, 2, K, F], F32, ctx)
            fsd = sb("fsd", [P, 2, 2, K, HID], F32, ctx)
            bl_out_b = sb("bl_out_b2", [P, F], F32, ctx)
            work = scratch[:, NCH * GROUP:NCH * GROUP + NK * F].rearrange("p (a f) -> p a f", f=F)
            sem = lambda n: ctx.enter_context(nc.semaphore(f"n1_{n}"))
            (staged, bias_loaded, turned, link_sem, var_ready, sqrt_done, x1_ready, x_turned, x_copied, f_summed,
             f_copied, r_copied) = map(sem, (
                "staged", "bias_loaded", "turned", "link", "var_ready", "sqrt_done", "x1_ready", "x_turned",
                "x_copied", "f_summed", "f_copied", "r_copied"))
            stored = [sem(f"stored{i}") for i in range(2)]
            flat_rest = rest[:, :, :, :].rearrange("p c k f -> p (c k) f")

            with ExitStack() as part:
                ps = part.enter_context(nc.psum_tensor("ps_agg", [P, NK, F], F32))
                block = part.enter_context(nc.Block())

                @block.sync
                def _(sp):
                    sp.dma_start(bl_out_b[:, :], bl_out.rearrange("(a f) -> a f", a=1).to_broadcast([P, F]))\
                      .then_inc(bias_loaded, 16)
                    sp.wait_ge(bias_loaded, 16)

                @block.tensor
                def _(pe):
                    for c in range(NCH):
                        for k in range(K):
                            t = pe.transpose(ps[:, c * K + k, :], table_b[0:F, c * GROUP + k:(c + 1) * GROUP:K],
                                             ident[0:F, 0:F])
                    t.then_inc(turned, 1)

                @block.scalar
                def _(act):
                    act.wait_ge(var_ready, 1)
                    act.activation(var[:, :], var[:, :], ACT.Sqrt).then_inc(sqrt_done, 1)

                @block.vector
                def _(dve):
                    link = Link(dve, link_sem)
                    link(dve.tensor_tensor(flat_nodes, flat_nodes, flat_rest, ALU.add))
                    dve.wait_ge(bias_loaded, 16)
                    link(dve.tensor_tensor(flat_nodes, flat_nodes, wide(bl_out_b[:, :], 1, [P, NK, F]), ALU.add))
                    dve.wait_ge(turned, 1)
                    link(dve.tensor_tensor(flat_nodes, flat_nodes, ps[:, :, :], ALU.add))
                    layer_norm(dve, var_ready, sqrt_done, link, flat_nodes, work, mean, var, flat_nodes)
                    dve.memset(xt[F:F + 1, :, :, :], 1.0)

            ps_x = [ctx.enter_context(nc.psum_tensor(f"ps_x1{i}", [F, K, P], F32)) for i in range(2)]
            ps_f = [ctx.enter_context(nc.psum_tensor(f"ps_f{i}", [P, K, 256], F32)) for i in range(2)]
            block = ctx.enter_context(nc.Block())
            WN = 2 * HID + F

            @block.tensor
            def _(pe):
                def step(c, par, lo, hi):
                    if inside(NCH, lo, hi, 0):
                        pe.wait_ge(staged, c + 1)
                        if lo >= 2:
                            pe.wait_ge(x_copied, c - 1)
                        for k in range(K):
                            t = pe.transpose(ps_x[par][:, k, :], stage[:, par, k, :], ident[:, :])
                        t.then_inc(x_turned, 1)
                    if inside(NCH, lo, hi, 1):
                        q = 1 - par
                        pe.wait_ge(x_copied, c)
                        if lo >= 3:
                            pe.wait_ge(f_copied, c - 2)
                            pe.wait_ge(r_copied, c - 2)
                        for k in range(K):
                            m = pe.matmul(ps_f[q][:, k, 0:WN], xt[:, q, k, :], w_node[:, :], start=True, stop=True)
                        m.then_inc(f_summed, 1)
                skewed(pe, NCH, 1, step)

            @block.scalar
            def _(act):
                def step(c, par, lo, hi):
                    if inside(NCH, lo, hi, 0):
                        act.wait_ge(x_turned, c + 1)
                        if lo >= 2:
                            act.wait_ge(f_summed, c - 1)
                        act.activation(xt[0:F, par, :, :], ps_x[par][:, :, :], ACT.Copy).then_inc(x_copied, 1)
                    if inside(NCH, lo, hi, 1):
                        q = 1 - par
                        act.wait_ge(f_summed, c)
                        if lo >= 3:
                            act.wait_ge(stored[q], (c - 2 + par) * 16)
                        act.activation(fsd[:, q, 0, :, :], ps_f[q][:, :, 0:HID], ACT.Copy)
                        act.activation(fsd[:, q, 1, :, :], ps_f[q][:, :, HID:2 * HID], ACT.Copy).then_inc(f_copied, 1)
                skewed(act, NCH, 1, step)

            @block.vector
            def _(dve):
                def step(c, par, lo, hi):
                    if inside(NCH, lo, hi, 0):
                        if lo >= 2:
                            dve.wait_ge(x_turned, c - 1)
                        dve.tensor_copy(stage[:, par, :, :], nodes[:, bass.ds(c, 1), :, :]
                                        .rearrange("p c k f -> p (c k) f")).then_inc(staged, 1)
                    if inside(NCH, lo, hi, 1):
                        dve.wait_ge(f_copied, c)
                        dve.tensor_tensor(rest[:, bass.ds(c - 1, 1), :, :].rearrange("p c k f -> p (c k) f"),
                                          nodes[:, bass.ds(c - 1, 1), :, :].rearrange("p c k f -> p (c k) f"),
                                          ps_f[1 - par][:, :, 2 * HID:WN], ALU.add).then_inc(r_copied, 1)
                skewed(dve, NCH, 1, step)

            @block.sync
            def _(sp):
                def step(c, par, lo, hi):
                    if inside(NCH, lo, hi, 0):
                        sp.wait_ge(f_copied, c + 1)
                        for which, table in enumerate((fs_dram, fd_dram)):
                            sp.dma_start(table[bass.ds(c * GROUP, GROUP), :].rearrange("(p k) f -> p (k f)", k=K),
                                         fsd[:, par, which, :, :].rearrange("p k f -> p (k f)")).then_inc(stored[par], 16)
                skewed(sp, NCH, 0, step)
                sp.wait_ge(stored[0], (NCH + 1) // 2 * 32)
                sp.wait_ge(stored[1], NCH // 2 * 32)

        with ExitStack() as ctx:
            oht = scratch[:, 0:2 * ST * P].rearrange("n (b t e) -> n b t e", b=2, t=ST)
            act_in = scratch[:, 2048:2048 + ST * HID].rearrange("p (t f) -> p t f", f=HID)
            fdw = sb("fdw", [WINDOW, SLOTS, SG, HID], F32, ctx)
            ps_o = [ctx.enter_context(nc.psum_tensor(f"ps_o{i}", [WINDOW, ST, P], F32)) for i in range(2)]
            ps_e = [ctx.enter_context(nc.psum_tensor(f"ps_e{i}", [P, ST, HID], F32)) for i in range(2)]
            sem = lambda n: ctx.enter_context(nc.semaphore(f"e_{n}"))
            idx_staged = [sem(f"idx_staged{s}") for s in range(SLOTS)]
            gathered = [sem(f"gathered{s}") for s in range(SLOTS)]
            fd_loaded = [sem(f"fd_loaded{s}") for s in range(SLOTS)]
            en_stored = [sem(f"en_stored{s}") for s in range(SLOTS)]
            rows_added = [sem(f"rows_added{s}") for s in range(SLOTS)]
            spread = [sem(f"spread{s}") for s in range(SLOTS)]
            onehot_ready, turned, link_sem, opened = map(sem, ("onehot_ready", "turned", "link", "opened"))
            copied = [sem(f"copied{i}") for i in range(2)]
            block = ctx.enter_context(nc.Block())

            @block.scalar
            def _(act):
                def iteration(it, first):
                    for s in range(SLOTS):
                        par = s % 2
                        if not first:
                            act.wait_ge(gathered[s], it * (16 * ST))
                        act.activation(idx_buf[:, s, :],
                                       src_idx[:, bass.ds(it * IG + s * SG, SG), :].rearrange("p g k -> p (g k)"),
                                       ACT.Copy).then_inc(idx_staged[s], 1)
                        act.wait_ge(turned, it * SLOTS + s + 1)
                        if s >= 2 or not first:
                            act.wait_ge(spread[(s - 2) % SLOTS], it + (1 if s >= 2 else 0))
                        act.activation(oht[:, par, :, :], ps_o[par][:, :, :], ACT.Copy).then_inc(copied[par], 1)
                iterations(act, IT, iteration)

            @block.gpsimd
            def _(pool):
                def iteration(it, first):
                    for s in range(SLOTS):
                        pool.wait_ge(idx_staged[s], it + 1)
                        if not first:
                            pool.wait_ge(rows_added[s], it)
                        if not first:
                            pool.wait_ge(en_stored[s], it * 16)
                        pool.sem_inc(opened, 1)
                        for t in range(ST):
                            pool.indirect_dma_start(
                                out=gath[:, s, t, :], out_offset=None, in_=fs_dram,
                                in_offset=bass.IndirectOffsetOnAxis(ap=idx_buf[:, s, t:t + 1], axis=0),
                            ).then_inc(gathered[s], 16)
                iterations(pool, IT, iteration)

            @block.sync
            def _(sp):
                def iteration(it, first):
                    _, starts = nc.values_load_multi_w_load_instructions(
                        win[0:1, bass.ds(it * IG, IG)], engines=SP_ENGINE, min_val=0, max_val=N,
                        skip_runtime_bounds_check_because=CLAMPED)
                    for s in range(SLOTS):
                        if not first:
                            sp.wait_ge(spread[s], it)
                        for g in range(SG):
                            sp.dma_start(fdw[:, s, g, :], fd_dram[bass.ds(starts[s * SG + g], WINDOW), :])\
                              .then_inc(fd_loaded[s], 16)
                        sp.wait_ge(gathered[s], it * (16 * ST) + 16 * ST)
                        sp.dma_start(en_dram[bass.ds(it * SLOTS + s, 1), :, :].rearrange("a p f -> (a p) f"),
                                     gath[:, s, :, :].rearrange("p t f -> p (t f)")).then_inc(en_stored[s], 16)
                iterations(sp, IT, iteration)
                for s in range(SLOTS):
                    sp.wait_ge(en_stored[s], IT * 16)

            @block.tensor
            def _(pe):
                def turn(n_ready, par, n_copied):
                    pe.wait_ge(onehot_ready, n_ready)
                    if n_copied is not None:
                        pe.wait_ge(copied[par], n_copied)
                    for t in range(ST):
                        m = pe.transpose(ps_o[par][:, t, :], onehot[:, par, t, :], ident[:, :])
                    m.then_inc(turned, 1)

                turn(1, 0, None)
                def iteration(it, first):
                    for s in range(SLOTS):
                        par = s % 2
                        turn(it * SLOTS + s + 2, 1 - par, it * 2 + (s + 1) // 2 if s or not first else None)
                        pe.wait_ge(copied[par], it * 2 + s // 2 + 1)
                        pe.wait_ge(fd_loaded[s], it * (16 * SG) + 16 * SG)
                        if s >= 2 or not first:
                            pe.wait_ge(rows_added[(s - 2) % SLOTS], it + (1 if s >= 2 else 0))
                        for t in range(ST):
                            m = pe.matmul(ps_e[par][:, t, :], oht[:, par, t, :], fdw[:, s, t // K, :],
                                          start=True, stop=True)
                        m.then_inc(spread[s], 1)
                iterations(pe, IT, iteration)

            @block.vector
            def _(dve):
                link = Link(dve, link_sem)

                def make_onehot(par, first_group):
                    dve.tensor_tensor(
                        onehot[:, par, :, :], wide(iota[:, :], 1, [P, ST, WINDOW]),
                        wide(dst_rel[:, bass.ds(first_group, SG), :].rearrange("p g k -> p (g k)"), 2, [P, ST, WINDOW]),
                        ALU.is_equal).then_inc(onehot_ready, 1)

                make_onehot(0, 0)
                def iteration(it, first):
                    link.iteration(it, 3 * SLOTS, 0)
                    for s in range(SLOTS):
                        par = s % 2
                        if s or not first:
                            dve.wait_ge(turned, it * SLOTS + s)
                        make_onehot(1 - par, it * IG + (s + 1) * SG)
                        dve.wait_ge(gathered[s], it * (16 * ST) + 16 * ST)
                        dve.wait_ge(spread[s], it + 1)
                        last = dve.tensor_tensor(act_in, gath[:, s, :, :], ps_e[par][:, :, :], ALU.add)
                        last.then_inc(rows_added[s], 1)
                        dve.wait_ge(rows_added[s], it + 1)
                        link(dve.scalar_tensor_tensor(act_in, act_in, SLOPE, act_in, ALU.mult, ALU.max))
                        link(dve.tensor_tensor(act_in, act_in, wide(attn_sb[:, :], 1, [P, ST, HID]), ALU.mult))
                        link(dve.tensor_reduce(
                            e_tab[:, bass.ds(it * IG + s * SG, SG), :, :].rearrange("p g k h -> p (g k h)"),
                            act_in.rearrange("p t (h f) -> p (t h) f", h=H), AX.X, ALU.add))
                iterations(dve, IT, iteration)

        with ExitStack() as ctx:
            e_row = scratch[0:J, 0:H * LONG].rearrange("j (h q) -> j h q", h=H)
            f_row = scratch[0:J, H * LONG:2 * H * LONG].rearrange("j (h q) -> j h q", h=H)
            at = 2 * H * LONG
            cont = scratch[0:J, at:at + LONG + 1]
            cneg = scratch[0:J, at + LONG + 4:at + 2 * LONG + 5]
            isend = scratch[0:J, at + 2 * LONG + 8:at + 3 * LONG + 8]
            dst_i = sb("dst_i", [J, LONG + 1], I32, ctx)
            back = [gath[0:J, :, :, :].rearrange("p s t f -> p (s t f)"),
                    onehot[0:J, :, :, :].rearrange("p b t n -> p (b t n)")]
            firsts = sb("firsts", [J, 4], F32, ctx)
            rowd = sb("rowd", [1, 16, J + 2], F32, ctx)
            carry = sb("carry", [J, H], F32, ctx)
            ps_t = ctx.enter_context(nc.psum_tensor("ps_st", [P, 16, P], F32))
            ps_r = ctx.enter_context(nc.psum_tensor("ps_sr", [P, 4, P], F32))
            ps_c = ctx.enter_context(nc.psum_tensor("ps_sc", [P, 16], F32))
            sem = lambda n: ctx.enter_context(nc.semaphore(f"s_{n}"))
            pads_set, dst_loaded, link_sem, e_turned, e_copied, cols_ready, cols_turned, rows_ready, rows_turned, \
                exp_in, exp_done, a_ready, a_turned, a_copied = map(sem, (
                    "pads_set", "dst_loaded", "link", "e_turned", "e_copied", "cols_ready", "cols_turned",
                    "rows_ready", "rows_turned", "exp_in", "exp_done", "a_ready", "a_turned", "a_copied"))
            block = ctx.enter_context(nc.Block())
            FIRST, LAST, JOIN, NEXT, BOTH, BOTHN, NEGB, NEGBN, STATE, CIN, TMP, VAL = range(12)

            def row(n, lo=0, hi=J):
                return rowd[0:1, n, lo:hi]

            @block.sync
            def _(sp):
                sp.wait_ge(pads_set, 1)
                sp.dma_start(dst_i[0:FULLJ, 0:LONG], dst[0:FULLJ * LONG].rearrange("(j q) -> j q", q=LONG))\
                  .then_inc(dst_loaded, 16)
                sp.dma_start(dst_i[FULLJ:FULLJ + 1, 0:RESTJ],
                             dst[FULLJ * LONG:E].rearrange("(j q) -> j q", q=RESTJ)).then_inc(dst_loaded, 16)
                sp.dma_start(dst_i[0:FULLJ, LONG:LONG + 1], dst[LONG:E:LONG].rearrange("(j a) -> j a", a=1),
                             allow_slow_non_contiguous=True)\
                  .then_inc(dst_loaded, 16)
                sp.wait_ge(dst_loaded, 48)

            @block.tensor
            def _(pe):
                for h in range(H):
                    if h:
                        pe.wait_ge(e_copied, h)
                    for c in range(K):
                        for k in range(K):
                            m = pe.transpose(ps_t[0:J, c * K + k, :], e_tab[:, c:G:K, k, h], ident[:, :])
                    m.then_inc(e_turned, 1)
                pe.wait_ge(cols_ready, 1)
                for c in range(2):
                    m = pe.transpose(ps_r[0:1, c, 0:J], firsts[:, c:c + 1], ident[0:J, 0:J])
                m.then_inc(cols_turned, 1)
                for n in range(4):
                    pe.wait_ge(cols_ready, 2 + n)
                    for h in range(H):
                        m = pe.transpose(ps_r[0:1, h, 0:J], firsts[:, 2 + h:3 + h], ident[0:J, 0:J])
                    m.then_inc(cols_turned, 1)
                    pe.wait_ge(rows_ready, 1 + n)
                    for h in range(H):
                        m = pe.transpose(ps_c[0:J, h:h + 1], row(CIN + 2 * h), ident[0:1, 0:1])
                    m.then_inc(rows_turned, 1)
                for h in range(H):
                    pe.wait_ge(a_ready, h + 1)
                    if h:
                        pe.wait_ge(a_copied, h)
                    for c in range(K):
                        for k in range(K):
                            m = pe.transpose(ps_t[:, c * K + k, 0:J],
                                             e_row[:, h, c * GROUP + k:(c + 1) * GROUP:K], ident[0:J, 0:J])
                    m.then_inc(a_turned, 1)

            @block.scalar
            def _(act):
                act.wait_ge(exp_in, H)
                act.activation(e_row, e_row, ACT.Exp).then_inc(exp_done, 1)

            @block.vector
            def _(dve):
                link = Link(dve, link_sem)
                last = min(96, FULLJ // 32 * 32)
                link(dve.memset(dst_i[last:J, :], NOWHERE))
                dve.memset(dst_i[:, LONG:LONG + 1], NOWHERE + 1).then_inc(pads_set, 1)
                for h in range(H):
                    dve.wait_ge(e_turned, h + 1)
                    dve.tensor_copy(e_row[:, h, :].rearrange("j (c p k) -> j c k p", c=K, k=K),
                                    ps_t[0:J, :, :].rearrange("j (c k) p -> j c k p", c=K)).then_inc(e_copied, 1)
                dve.wait_ge(dst_loaded, 48)
                dve.tensor_copy(firsts[:, 0:1], dst_i[:, 0:1])
                dve.tensor_copy(firsts[:, 1:2], dst_i[:, LONG - 1:LONG]).then_inc(cols_ready, 1)
                dve.tensor_tensor(cont[:, 1:LONG], dst_i[:, 1:LONG], dst_i[:, 0:LONG - 1], ALU.is_equal)
                dve.memset(cont[:, 0:1], 1.0)
                link(dve.memset(cont[:, LONG:LONG + 1], 1.0))
                dve.tensor_scalar(cneg, cont, 1.0, BIG, ALU.subtract, ALU.mult)
                dve.tensor_tensor(isend, dst_i[:, 1:LONG + 1], dst_i[:, 0:LONG], ALU.not_equal)
                dve.wait_ge(cols_turned, 1)
                link(dve.memset(rowd[:, :, :], 0.0))
                link(dve.tensor_copy(rowd[0:1, FIRST:LAST + 1, 0:J], ps_r[0:1, 0:2, 0:J]))
                link(dve.tensor_tensor(row(TMP), row(FIRST), row(LAST), ALU.is_equal))
                link(dve.tensor_tensor(row(JOIN, 1), row(FIRST, 1), row(LAST, 0, J - 1), ALU.is_equal))
                link(dve.tensor_copy(row(NEXT, 0, J - 1), row(JOIN, 1)))
                link(dve.tensor_tensor(row(BOTH), row(TMP), row(JOIN), ALU.mult))
                link(dve.tensor_tensor(row(BOTHN), row(TMP), row(NEXT), ALU.mult))
                link(dve.tensor_scalar(row(NEGB), row(BOTH), 1.0, BIG, ALU.subtract, ALU.mult))
                link(dve.tensor_scalar(row(NEGBN), row(BOTHN), 1.0, BIG, ALU.subtract, ALU.mult))

                def carried(n, is_max, forward):
                    dve.wait_ge(cols_turned, 2 + n)
                    ident_value = -BIG if is_max else 0.0
                    for h in range(H):
                        state, cin = STATE, CIN + 2 * h
                        link(dve.tensor_copy(row(TMP), ps_r[0:1, h, 0:J]))
                        gate = row((NEGB if forward else NEGBN) if is_max else (BOTH if forward else BOTHN))
                        a, b, o = gate, row(TMP), row(state)
                        if not forward:
                            a, b, o = (v[:, ::-1] for v in (a, b, o))
                        link(dve.tensor_tensor_scan(o, a, b, ident_value, ALU.add if is_max else ALU.mult,
                                                    ALU.max if is_max else ALU.add))
                        link(dve.memset(row(cin), ident_value))
                        if forward:
                            to, came, gate = row(cin, 1), row(state, 0, J - 1), row(JOIN, 1)
                            minus = row(TMP, 1)
                        else:
                            to, came, gate = row(cin, 0, J - 1), row(state, 1), row(NEXT, 0, J - 1)
                            minus = row(TMP, 0, J - 1)
                        link(dve.tensor_tensor(to, came, gate, ALU.mult))
                        if is_max:
                            link(dve.tensor_scalar(minus, gate, 1.0, BIG, ALU.subtract, ALU.mult))
                            link(dve.tensor_tensor(to, to, minus, ALU.add))
                    dve.tensor_copy(row(TMP), row(TMP)).then_inc(rows_ready, 1)
                    dve.wait_ge(rows_turned, 1 + n)
                    link(dve.tensor_copy(carry[:, :], ps_c[0:J, 0:H]))

                def totals(n, is_max):
                    op0, op1 = (ALU.add, ALU.max) if is_max else (ALU.mult, ALU.add)
                    gates = cneg if is_max else cont
                    start = -BIG if is_max else 0.0
                    for h in range(H):
                        link(dve.tensor_tensor_scan(f_row[:, h, :], gates[:, 0:LONG], e_row[:, h, :], start, op0, op1))
                        link(dve.tensor_copy(firsts[:, 2 + h:3 + h], f_row[:, h, LONG - 1:LONG]))
                    dve.tensor_copy(firsts[:, 0:1], firsts[:, 0:1]).then_inc(cols_ready, 1)
                    carried(n, is_max, True)
                    for h in range(H):
                        link(dve.tensor_tensor_scan(f_row[:, h, :], gates[:, 0:LONG], e_row[:, h, :],
                                                    carry[:, h:h + 1], op0, op1))
                        if not is_max:
                            link(dve.tensor_tensor(f_row[:, h, :], f_row[:, h, :], isend, ALU.mult))
                        b_row = back[h]
                        link(dve.tensor_tensor_scan(b_row[:, ::-1], gates[:, 1:LONG + 1][:, ::-1],
                                                    f_row[:, h, ::-1], start, op0, op1))
                        link(dve.tensor_copy(firsts[:, 2 + h:3 + h], b_row[:, 0:1]))
                    dve.tensor_copy(firsts[:, 0:1], firsts[:, 0:1]).then_inc(cols_ready, 1)
                    carried(n + 1, is_max, False)
                    for h in range(H):
                        link(dve.tensor_tensor_scan(back[h][:, ::-1], gates[:, 1:LONG + 1][:, ::-1],
                                                    f_row[:, h, ::-1], carry[:, h:h + 1], op0, op1))

                totals(0, True)
                for h in range(H):
                    dve.tensor_tensor(e_row[:, h, :], e_row[:, h, :], back[h], ALU.subtract).then_inc(exp_in, 1)
                dve.wait_ge(exp_done, 1)
                totals(2, False)
                for h in range(H):
                    link(dve.tensor_scalar(back[h], back[h], 1e-9, None, ALU.max))
                    link(dve.reciprocal(back[h], back[h]))
                    dve.tensor_tensor(e_row[:, h, :], e_row[:, h, :], back[h], ALU.mult).then_inc(a_ready, 1)
                for h in range(H):
                    dve.wait_ge(a_turned, h + 1)
                    dve.tensor_copy(e_tab[:, :, :, h].rearrange("p (j c) k -> p j (c k)", c=K),
                                    ps_t[:, :, 0:J].rearrange("p a j -> p j a")).then_inc(a_copied, 1)

        with ExitStack() as ctx:
            en = scratch[:, 0:SLOTS * ST * HID].rearrange("p (s t f) -> p s t f", s=SLOTS, t=ST)
            r = scratch[:, SLOTS * ST * HID:2 * SLOTS * ST * HID].rearrange("p (s t f) -> p s t f", s=SLOTS, t=ST)
            top = sb("top", [P, SLOTS, ST * H], F32, ctx)
            total = sb("total", [P, SLOTS, ST * H], F32, ctx)
            ps = [ctx.enter_context(nc.psum_tensor(f"m_ps{i}", [HID, SG, WINDOW], F32)) for i in range(2)]
            sem = lambda n: ctx.enter_context(nc.semaphore(f"m_{n}"))
            loaded = [sem(f"loaded{s}") for s in range(SLOTS)]
            (multiplied, top_ready, centred, scaled, exp_done, sum_ready, rec_ready, msg_ready, onehot_ready, summed,
             added) = map(sem, ("multiplied", "top_ready", "centred", "scaled", "exp_done", "sum_ready", "rec_ready",
                                "msg_ready", "onehot_ready", "summed", "added"))
            NS = IT * SLOTS
            block = ctx.enter_context(nc.Block())
            r_view = edge_attr.rearrange("e h f -> e (h f)")

            def heads(ap):
                return ap.rearrange("p t (h f) -> p (t h) f", h=H)

            @block.sync
            def _(sp):
                def load(n, s, edges):
                    sp.dma_start(en[:, s, :, :].rearrange("p t f -> p (t f)"),
                                 en_dram[bass.ds(n, 1), :, :].rearrange("a p f -> (a p) f")).then_inc(loaded[s], 16)
                    for g in range(SG):
                        parts = P if edges is None else min(P, max(0, edges - g * GROUP) // K)
                        if parts:
                            sp.dma_start(r[0:parts, s, g * K:(g + 1) * K, :].rearrange("p t f -> p (t f)"),
                                         r_view[bass.ds((n * SG + g) * GROUP, parts * K), :]
                                         .rearrange("(p k) f -> p (k f)", k=K)).then_inc(loaded[s], 16)

                def step(n, s, lo, hi):
                    if lo >= SLOTS:
                        sp.wait_ge(summed, n - (SLOTS - 1))
                    load(n, s, None if lo != hi else E - n * SG * GROUP)

                skewed(sp, NS, 0, step, SLOTS, SLOTS)

            def arrived(n, s, lo, hi):
                if lo != hi:
                    return (n - s + SLOTS) * (16 * (1 + SG) // SLOTS)
                count = 0
                for m in range(s, n + 1, SLOTS):
                    count += 16
                    for g in range(SG):
                        count += 16 * (E - (m * SG + g) * GROUP >= K)
                return count

            @block.vector
            def _(dve):
                starts = []

                def load_starts(first_group):
                    starts[:] = nc.values_load_multi_w_load_instructions(
                        win[0:1, bass.ds(first_group, IG)], engines=DVE_ENGINE, min_val=0, max_val=N,
                        skip_runtime_bounds_check_because=CLAMPED)[1]

                def step(n, s, lo, hi):
                    if inside(NS, lo, hi, 0):
                        dve.wait_ge(loaded[s], arrived(n, s, lo, hi))
                        dve.tensor_tensor(en[:, s, :, :], en[:, s, :, :], r[:, s, :, :], ALU.mult)\
                           .then_inc(multiplied, 1)
                        dve.wait_ge(multiplied, n + 1)
                        dve.tensor_reduce(top[:, s, :], heads(en[:, s, :, :]), AX.X, ALU.max).then_inc(top_ready, 1)
                    if inside(NS, lo, hi, 1):
                        q = (s - 1) % SLOTS
                        if lo >= 3:
                            dve.wait_ge(summed, n - 2)
                        dve.tensor_tensor(
                            onehot[:, q % 2, :, :], wide(iota[:, :], 1, [P, ST, WINDOW]),
                            wide(dst_rel[:, bass.ds((n - 1) * SG, SG), :].rearrange("p g k -> p (g k)"), 2,
                                 [P, ST, WINDOW]), ALU.is_equal).then_inc(onehot_ready, 1)
                        dve.wait_ge(exp_done, n)
                        dve.tensor_reduce(total[:, q, :], heads(en[:, q, :, :]), AX.X, ALU.add).then_inc(sum_ready, 1)
                        dve.wait_ge(sum_ready, n)
                        dve.reciprocal(total[:, q, :], total[:, q, :]).then_inc(rec_ready, 1)
                    if inside(NS, lo, hi, 2):
                        base = (n - 2) * SG % IG if lo == hi else s * SG
                        if lo == hi and n == 2:
                            load_starts(0)
                        if lo == hi and n >= NS - 2 and n % SLOTS in (0, 2) or lo == hi and n == NS - SLOTS:
                            load_starts((n - 2) * SG - (n - 2) * SG % IG)
                        if lo != hi and s == 0:
                            load_starts((n - 2) * SG)
                        dve.wait_ge(summed, n - 1)
                        for g in range(SG):
                            dve.wait_ge(added, (n - 2) * SG + g)
                            to = table_a[0:HID, bass.ds(starts[base + g], WINDOW)]
                            dve.tensor_tensor(to, to, ps[s % 2][:, g, :], ALU.add).then_inc(added, 1)
                skewed(dve, NS, 2, step, SLOTS, SLOTS)

            @block.gpsimd
            def _(pool):
                def step(n, s, lo, hi):
                    if inside(NS, lo, hi, 0):
                        rows = heads(en[:, s, :, :])
                        pool.wait_ge(top_ready, n + 1)
                        pool.tensor_tensor(rows, rows, wide(top[:, s, :], 2, [P, ST * H, F]), ALU.subtract)\
                            .then_inc(centred, 1)
                        pool.wait_ge(centred, n + 1)
                        weights = e_tab[:, bass.ds(n * SG, SG), :, :].rearrange("p g k h -> p (g k h)")
                        pool.tensor_tensor(rows, rows, wide(weights, 2, [P, ST * H, F]), ALU.mult)\
                            .then_inc(scaled, 1)
                    if inside(NS, lo, hi, 1):
                        q = (s - 1) % SLOTS
                        rows = heads(en[:, q, :, :])
                        pool.wait_ge(rec_ready, n)
                        pool.tensor_tensor(rows, rows, wide(total[:, q, :], 2, [P, ST * H, F]), ALU.mult)\
                            .then_inc(msg_ready, 1)
                skewed(pool, NS, 1, step, SLOTS)

            @block.scalar
            def _(act):
                def step(n, s, lo, hi):
                    act.wait_ge(scaled, n + 1)
                    act.activation(en[:, s, :, :], en[:, s, :, :], ACT.Exp).then_inc(exp_done, 1)
                skewed(act, NS, 0, step, SLOTS)

            @block.tensor
            def _(pe):
                def step(n, s, lo, hi):
                    par = s % 2
                    pe.wait_ge(msg_ready, n + 1)
                    pe.wait_ge(onehot_ready, n + 1)
                    if lo >= 2:
                        pe.wait_ge(added, (n - 1) * SG)
                    for g in range(SG):
                        for k in range(K):
                            m = pe.matmul(ps[par][:, g, :], en[:, s, g * K + k, :], onehot[:, par, g * K + k, :],
                                          start=(k == 0), stop=(k == K - 1))
                    m.then_inc(summed, 1)
                skewed(pe, NS, 0, step, SLOTS)

        with ExitStack() as ctx:
            mean = sb("mean2", [P, NK], F32, ctx)
            var = sb("var2", [P, NK], F32, ctx)
            work = scratch[:, 0:NK * F].rearrange("p (a f) -> p a f", f=F)
            flat_rest = rest[:, :, :, :].rearrange("p c k f -> p (c k) f")
            ps = ctx.enter_context(nc.psum_tensor("ps_out", [P, NK, F], F32))
            sem = lambda n: ctx.enter_context(nc.semaphore(f"o_{n}"))
            projected, link_sem, var_ready, sqrt_done, out_ready, stored = map(sem, (
                "projected", "link", "var_ready", "sqrt_done", "out_ready", "stored"))
            block = ctx.enter_context(nc.Block())

            @block.tensor
            def _(pe):
                for c in range(NCH):
                    for k in range(K):
                        m = pe.matmul(ps[:, c * K + k, :], table_a[0:HID, c * GROUP + k:(c + 1) * GROUP:K],
                                      w1_twice[:, :], start=True, stop=True)
                m.then_inc(projected, 1)

            @block.scalar
            def _(act):
                act.wait_ge(var_ready, 1)
                act.activation(var[:, :], var[:, :], ACT.Sqrt).then_inc(sqrt_done, 1)

            @block.vector
            def _(dve):
                link = Link(dve, link_sem)
                dve.wait_ge(projected, 1)
                link(dve.tensor_tensor(flat_rest, flat_rest, ps[:, :, :], ALU.add))
                layer_norm(dve, var_ready, sqrt_done, link, flat_rest, work, mean, var, flat_nodes)
                dve.memset(mean[:, 0:1], 0.0).then_inc(out_ready, 1)

            @block.sync
            def _(sp):
                sp.wait_ge(out_ready, 1)
                full = N // GROUP
                sp.dma_start(out[0:full * GROUP, :].rearrange("(c p k) f -> p c (k f)", p=P, k=K),
                             nodes[:, 0:full, :, :].rearrange("p c k f -> p c (k f)")).then_inc(stored, 16)
                left = (N - full * GROUP) // K
                sp.dma_start(out[full * GROUP:N, :].rearrange("(p k) f -> p (k f)", k=K),
                             nodes[0:left, full, :, :].rearrange("p k f -> p (k f)")).then_inc(stored, 16)
                sp.wait_ge(stored, 32)


_INS = ["x", "src", "dst", "edge_attr3_2x32", "L0_gnn_W_l_in", "L0_gnn_b_l_in", "L0_gnn_W_r_in", "L0_gnn_W_l_out",
        "L0_gnn_b_l_out", "L0_gnn_W_r_out", "L1_gnn_W1", "L1_gnn_b1", "L1_gnn_W2s", "L1_gnn_b2s", "L1_gnn_W2d",
        "L1_gnn_b2d", "L1_gnn_attn"]


def kernel(**inputs):
    import numpy as np
    import concourse.bacc as bacc
    from concourse.bass_utils import run_bass_kernel_spmd

    nc = bacc.Bacc("TRN2", target_bir_lowering=False, num_devices=1)
    arrays, args = {}, []
    for name in _INS:
        a = np.ascontiguousarray(inputs[name])
        arrays[f"in_{name}"] = a
        args.append(nc.dram_tensor(f"in_{name}", a.shape, mybir.dt.from_np(a.dtype), kind="ExternalInput").ap())
    out = nc.dram_tensor("out", arrays["in_x"].shape, F32, kind="ExternalOutput").ap()
    build(nc, *args, out)
    return run_bass_kernel_spmd(nc, [arrays], core_ids=[0]).results[0]["out"]
```

```python
import concourse.bass as bass
from concourse import mybir
from concourse.alu_op_type import AluOpType as ALU
from contextlib import ExitStack

F32 = mybir.dt.float32
I32 = mybir.dt.int32
ACT = mybir.ActivationFunctionType
AX = mybir.AxisListType
DVE_ENGINE = [mybir.EngineType.DVE]
SP_ENGINE = [mybir.EngineType.SP]

P = 128
HEAD = 4
K = 4
GROUP = P * K
WINDOW = 128
SLOTS = 4
SG = 2
ST = SG * K
IG = SLOTS * SG
F = 32
HID = 64
H = 2
ROW = HID + H
PART = 7
BEFORE = 3
SROWS = 64
BIG = 1.0e38
EPS = 1e-5
SLOPE = 0.2
CLAMPED = "set-up clamps the starts"
NOWHERE = 1 << 20


def sizes(n_nodes, n_edges):
    iters = -(-n_edges // (GROUP * IG))
    groups = iters * IG
    rows = groups // K
    chunks = -(-(n_nodes + WINDOW) // GROUP)
    return iters, groups, rows, chunks


def iterations(engine, count, body):
    body(0, True)
    with engine.Fori(1, count) as it:
        body(it, False)


class Link:

    def __init__(self, engine, sem):
        self.engine, self.sem, self.count, self.base = engine, sem, 0, 0

    def __call__(self, instruction):
        instruction.then_inc(self.sem, 1)
        self.count += 1
        self.engine.wait_ge(self.sem, self.base + self.count)

    def iteration(self, i, per_iteration, before):
        self.base, self.count = i * per_iteration + before, 0

    def after(self, total):
        self.base, self.count = 0, total


def wide(ap, at, shape):
    return ap.unsqueeze(at).to_broadcast(shape)


def build(nc, x, src, dst, edge_attr, wl_in, bl_in, wr_in, wl_out, bl_out, wr_out,
          w1, b1, w2s, b2s, w2d, b2d, attn, out):
    N, E = x.shape[0], src.shape[0]
    IT, G, J, NCH = sizes(N, E)
    LONG = K * GROUP
    NK = NCH * K
    FULLJ, RESTJ = E // LONG, E % LONG
    assert J <= P and RESTJ % K == 0 and N % K == 0

    y_dram = nc.dram_tensor("y_scratch", (NCH * GROUP, F), F32, kind="Internal").ap()
    fs_dram = nc.dram_tensor("fs_scratch", (NCH * GROUP, ROW), F32, kind="Internal").ap()
    fd_dram = nc.dram_tensor("fd_scratch", (NCH * GROUP, ROW), F32, kind="Internal").ap()
    en_dram = nc.dram_tensor("en_scratch", (IT * SLOTS, P, ST * ROW), F32, kind="Internal").ap()
    dst_dram = nc.dram_tensor("dst_scratch", ((BEFORE + G + SROWS + 1) * GROUP,), I32, kind="Internal").ap()

    dcol_dram = nc.dram_tensor("dst_columns", (P, G * K), F32, kind="Internal").ap()
    drow_dram = nc.dram_tensor("dst_rows", (J, LONG), F32, kind="Internal").ap()
    e_dram = nc.dram_tensor("scores_scratch", (G * GROUP, H), F32, kind="Internal").ap()
    nd_dram = nc.dram_tensor("stats_scratch", (NCH * GROUP, 2 * H), F32, kind="Internal").ap()

    def skewed(engine, chunks, lags, step, unroll=2, peel=0):
        loops = (chunks - HEAD - peel) // unroll
        for c in range(HEAD):
            step(c, c % unroll, c, c)
        with engine.Fori(0, loops) as i:
            for u in range(unroll):
                step(i * unroll + (HEAD + u), u, HEAD, chunks - 1)
        for c in range(HEAD + unroll * loops, chunks + lags):
            step(c, c % unroll, c, c)

    def inside(chunks, lo, hi, lag):
        return lo - lag >= 0 and hi - lag < chunks

    with ExitStack() as whole:
        def sb(name, shape, dt=F32, ctx=whole):
            return ctx.enter_context(nc.sbuf_tensor(name, shape, dt))

        by_slot = {stage: [whole.enter_context(nc.semaphore(f"{stage}_gathered{s}")) for s in range(SLOTS)]
                   for stage in ("sum_x", "sum_y", "scores")}
        alone = {stage: whole.enter_context(nc.semaphore(f"{stage}_gathered"))
                 for stage in ("all_x", "all_y", "scores", "messages")}
        spent = []

        def new_sem(ctx, name):
            sem = ctx.enter_context(nc.semaphore(name))
            spent.append(sem.num)
            return sem

        def reset_semaphores():
            with nc.Block() as block:
                @block.vector
                def _(dve):
                    dve.sem_clear(range(min(spent), max(spent) + 1))
            spent.clear()

        ident = sb("ident", [P, P])
        iota = sb("iota", [P, WINDOW])
        ones = sb("ones", [1, P])
        attn_sb = sb("attn_sb", [P, HID])
        wl_in_t = sb("wl_in_t", [F, P])
        wr_in_t = sb("wr_in_t", [F, P])
        b_in = sb("b_in", [HID, 1])
        w_out_t = sb("w_out_t", [HID, HID])
        w_node = sb("w_node", [F + 1, 2 * ROW + F])
        w1_twice = sb("w1_twice", [HID, F])
        table_a = sb("table_a", [P, NCH * GROUP])
        scratch = sb("scratch", [P, 16400])
        nodes = sb("nodes", [P, NCH, K, F])
        rest = sb("rest", [P, NCH, K, F])
        src_idx = sb("src_idx", [P, G + IG, K], I32)
        dst_rel = sb("dst_rel", [P, G + SG, K])
        e_tab = sb("e_tab", [P, BEFORE + G + SROWS, K, H])
        win = sb("win", [1, G], I32)
        general = sb("general", [1, 1], I32)
        attn_whole = sb("attn_whole", [P, HID])
        gath = sb("gath", [P, SLOTS, ST, ROW])
        idx_buf = sb("idx_buf", [P, SLOTS, ST], I32)
        onehot = sb("onehot", [P, 2, ST, WINDOW])
        flat_nodes = nodes[:, :, :, :].rearrange("p c k f -> p (c k) f")
        table_b = scratch[:, 0:NCH * GROUP]

        with ExitStack() as ctx:
            rows_i = scratch[:, 0:LONG].bitcast(I32)
            rows_f = scratch[:, LONG:3 * LONG].rearrange("p (w q) -> p w q", w=2)
            iota_i = sb("iota_i", [P, P], I32, ctx)
            pid_i = sb("pid_i", [P, 1], I32, ctx)
            pid = sb("pid", [P, 1], F32, ctx)
            dst_col = sb("dst_col", [P, G, K], F32, ctx)
            win_f = sb("win_f", [1, G], F32, ctx)
            bl_out_b = sb("bl_out_b", [P, F], F32, ctx)
            w_rows = sb("w_rows", [HID, 4, HID], F32, ctx)
            lead = sb("lead", [P, BEFORE * GROUP // P], I32, ctx)
            trail = sb("trail", [P, (SROWS + 1) * GROUP // P], I32, ctx)
            linear = sb("linear", [F + 1, HID], F32, ctx)
            around_set = new_sem(ctx, "around_set")
            after_i = sb("after_i", [P, 1], I32, ctx)
            after_f = sb("after_f", [P, 1], F32, ctx)
            mark = sb("mark", [1, 1], F32, ctx)
            lowest = sb("lowest", [P, 1], F32, ctx)
            bad = sb("bad", [P, 4], F32, ctx)
            steps = scratch[:, 3 * LONG:4 * LONG]
            reach = scratch[:, 4 * LONG:4 * LONG + G * K]
            bad_row = sb("bad_row", [1, P], F32, ctx)
            ps_t = ctx.enter_context(nc.psum_tensor("ps_t", [P, 16, P], F32))
            ps_w = ctx.enter_context(nc.psum_tensor("ps_w", [P, 4, P], F32))
            ps_b = ctx.enter_context(nc.psum_tensor("ps_b", [P, 512], F32))
            pads_set = new_sem(ctx, "pads_set")
            src_loaded = new_sem(ctx, "src_loaded")
            dst_loaded = new_sem(ctx, "dst_loaded")
            x_loaded = new_sem(ctx, "x_loaded")
            w_loaded = new_sem(ctx, "w_loaded")
            iotas = new_sem(ctx, "iotas")
            consts = new_sem(ctx, "consts")
            src_used = new_sem(ctx, "src_used")
            link_sem = new_sem(ctx, "setup_link")
            rows_ready = new_sem(ctx, "rows_ready")
            turned = new_sem(ctx, "turned")
            turned_used = new_sem(ctx, "turned_used")
            w_turned = new_sem(ctx, "w_turned")
            after_loaded, copies_stored, cols_made, bad_ready, bad_turned = (
                new_sem(ctx, n) for n in ("after_loaded", "copies_stored", "cols_made",
                                                             "bad_ready", "bad_turned"))
            win_ready = new_sem(ctx, "win_ready")
            win_spread = new_sem(ctx, "win_spread")
            block = ctx.enter_context(nc.Block())

            @block.gpsimd
            def _(pool):
                pool.iota(iota_i[:, :], [[1, P]], base=0, channel_multiplier=0).then_inc(iotas, 1)
                pool.iota(pid_i[:, :], [[0, 1]], base=0, channel_multiplier=1).then_inc(iotas, 1)
                pool.memset(nodes[:, N // GROUP:NCH, :, :], 0.0).then_inc(pads_set, 1)
                pool.memset(w_node[:, :], 0.0).then_inc(pads_set, 1)
                pool.memset(lead[:, :], -1).then_inc(around_set, 1)
                pool.memset(trail[:, :], NOWHERE).then_inc(around_set, 1)
                pool.memset(e_tab[:, :, :, :], 0.0)

            @block.sync
            def _(sp):
                sp.wait_ge(consts, 1)
                sp.dma_start(rows_i[0:FULLJ, :], src[0:FULLJ * LONG].rearrange("(j q) -> j q", q=LONG))\
                  .then_inc(src_loaded, 16)
                sp.dma_start(rows_i[FULLJ:FULLJ + 1, 0:RESTJ],
                             src[FULLJ * LONG:E].rearrange("(j q) -> j q", q=RESTJ)).then_inc(src_loaded, 16)
                sp.wait_ge(pads_set, 2)
                full = N // GROUP
                sp.dma_start(nodes[:, 0:full, :, :].rearrange("p c k f -> p c (k f)"),
                             x[0:full * GROUP, :].rearrange("(c p k) f -> p c (k f)", p=P, k=K)).then_inc(x_loaded, 16)
                left = (N - full * GROUP) // K
                sp.dma_start(nodes[0:left, full, :, :].rearrange("p k f -> p (k f)"),
                             x[full * GROUP:N, :].rearrange("(p k) f -> p (k f)", k=K)).then_inc(x_loaded, 16)
                sp.wait_ge(consts, 3)
                sp.dma_start(rows_i[0:FULLJ, :], dst[0:FULLJ * LONG].rearrange("(j q) -> j q", q=LONG))\
                  .then_inc(dst_loaded, 16)
                sp.dma_start(rows_i[FULLJ:FULLJ + 1, 0:RESTJ],
                             dst[FULLJ * LONG:E].rearrange("(j q) -> j q", q=RESTJ)).then_inc(dst_loaded, 16)
                sp.dma_start(after_i[0:FULLJ, :], dst[LONG:E:LONG].rearrange("(j a) -> j a", a=1),
                             allow_slow_non_contiguous=True).then_inc(after_loaded, 16)
                sp.wait_ge(rows_ready, 1)
                sp.dma_start(drow_dram, rows_f[0:J, 1, :]).then_inc(copies_stored, 16)
                sp.wait_ge(cols_made, 1)
                sp.dma_start(dcol_dram, dst_col[:, :, :].rearrange("p g k -> p (g k)")).then_inc(copies_stored, 16)
                sp.wait_ge(around_set, 2)
                at = BEFORE * GROUP
                sp.dma_start(dst_dram[0:at].rearrange("(p q) -> p q", p=P), lead[:, :]).then_inc(copies_stored, 16)
                sp.dma_start(dst_dram[at:at + J * LONG].rearrange("(j q) -> j q", q=LONG), rows_i[0:J, :])\
                  .then_inc(copies_stored, 16)
                sp.dma_start(dst_dram[at + J * LONG:].rearrange("(p q) -> p q", p=P), trail[:, :])\
                  .then_inc(copies_stored, 16)
                sp.wait_ge(copies_stored, 80)
                sp.wait_ge(src_loaded, 32)
                sp.wait_ge(dst_loaded, 32)
                sp.wait_ge(after_loaded, 16)
                sp.wait_ge(x_loaded, 32)

            @block.scalar
            def _(act):
                act.dma_start(w_rows[0:HID, 0, 0:F], wl_in).then_inc(w_loaded, 16)
                act.dma_start(w_rows[0:HID, 1, 0:F], wr_in).then_inc(w_loaded, 16)
                act.dma_start(w_rows[0:F, 2, :], wl_out).then_inc(w_loaded, 16)
                act.dma_start(w_rows[0:F, 3, :], wr_out).then_inc(w_loaded, 16)
                act.dma_start(b_in[:, :], bl_in.rearrange("(f a) -> f a", a=1)).then_inc(w_loaded, 16)
                act.dma_start(bl_out_b[:, :], bl_out.rearrange("(a f) -> a f", a=1).to_broadcast([P, F])).then_inc(w_loaded, 16)
                act.dma_start(attn_sb[:, :], attn.rearrange("a h f -> a (h f)").to_broadcast([P, HID])).then_inc(w_loaded, 16)
                act.wait_ge(pads_set, 2)
                act.dma_start(w_node[0:F, 0:HID], w2s).then_inc(w_loaded, 16)
                act.dma_start(w_node[0:F, ROW:ROW + HID], w2d).then_inc(w_loaded, 16)
                act.dma_start(w_node[0:F, 2 * ROW:2 * ROW + F], w1).then_inc(w_loaded, 16)
                act.dma_start(w_node[F:F + 1, 0:HID], b2s.rearrange("(a f) -> a f", a=1)).then_inc(w_loaded, 16)
                act.dma_start(w_node[F:F + 1, ROW:ROW + HID], b2d.rearrange("(a f) -> a f", a=1)).then_inc(w_loaded, 16)
                act.dma_start(w_node[F:F + 1, 2 * ROW:2 * ROW + F], b1.rearrange("(a f) -> a f", a=1)).then_inc(w_loaded, 16)
                act.dma_start(w1_twice[0:F, :], w1).then_inc(w_loaded, 16)
                act.dma_start(w1_twice[F:HID, :], w1).then_inc(w_loaded, 16)
                act.wait_ge(w_loaded, 15 * 16)

            @block.vector
            def _(dve):
                link = Link(dve, link_sem)
                last = min(96, FULLJ // 32 * 32)
                link(dve.memset(rows_i[last:P, :], 0))
                dve.memset(ones[:, :], 1.0).then_inc(consts, 1)
                dve.wait_ge(iotas, 2)
                dve.tensor_copy(iota[:, :], iota_i[:, 0:WINDOW])
                link(dve.tensor_copy(pid[:, :], pid_i[:, :]))
                dve.memset(table_a[:, :], 0.0)
                dve.memset(wl_in_t[:, :], 0.0)
                dve.memset(wr_in_t[:, :], 0.0)
                link(dve.tensor_scalar(ident[:, :], iota_i[:, :], pid[:, 0:1], None, ALU.is_equal))
                dve.wait_ge(src_loaded, 32)
                link(dve.tensor_copy(rows_f[0:J, 0, :], rows_i[0:J, :]))
                dve.memset(ones[:, :], 1.0).then_inc(consts, 1)
                link(dve.memset(rows_i[last:P, :], NOWHERE))
                link(dve.memset(after_i[:, :], NOWHERE))
                link(dve.memset(bad[:, :], 0.0))
                dve.memset(ones[:, :], 1.0).then_inc(consts, 1)
                dve.wait_ge(dst_loaded, 32)
                link(dve.tensor_copy(rows_f[0:J, 1, :], rows_i[0:J, :]))
                dve.memset(ones[:, :], 1.0).then_inc(rows_ready, 1)
                dve.wait_ge(turned, 1)
                dve.tensor_copy(src_idx[:, 0:G, :].rearrange("p (j c) k -> p j (c k)", c=K),
                                ps_t[:, :, 0:J].rearrange("p a j -> p j a")).then_inc(turned_used, 1)
                dve.memset(src_idx[:, G:G + IG, :], 0)
                dve.wait_ge(turned, 2)
                link(dve.tensor_copy(dst_col[:, :, :].rearrange("p (j c) k -> p j (c k)", c=K),
                                     ps_t[:, :, 0:J].rearrange("p a j -> p j a")))
                link(dve.tensor_scalar(win_f[:, :], dst_col[0:1, :, 0], float(N), None, ALU.min))
                dve.tensor_copy(win[:, :], win_f[:, :]).then_inc(win_ready, 1)
                dve.memset(mark[:, :], 1.0).then_inc(cols_made, 1)
                dve.wait_ge(win_spread, 1)
                dve.tensor_tensor(dst_rel[:, 0:G, :], dst_col[:, :, :],
                                  wide(ps_b[:, 0:G], 2, [P, G, K]), ALU.subtract)
                dve.memset(dst_rel[:, G:G + SG, :], float(NOWHERE))
                dve.wait_ge(after_loaded, 16)
                link(dve.tensor_copy(after_f[:, :], after_i[:, :]))
                link(dve.tensor_tensor(steps[0:J, 0:LONG - 1], rows_f[0:J, 1, 1:LONG], rows_f[0:J, 1, 0:LONG - 1],
                                       ALU.subtract))
                link(dve.tensor_tensor(steps[0:J, LONG - 1:LONG], after_f[0:J, :], rows_f[0:J, 1, LONG - 1:LONG],
                                       ALU.subtract))
                link(dve.tensor_reduce(lowest[0:J, :], steps[0:J, :], AX.X, ALU.min))
                link(dve.tensor_scalar(bad[0:J, 0:1], lowest[0:J, :], 0.0, None, ALU.is_lt))
                real = dst_rel[:, 0:G, :].rearrange("p g k -> p (g k)")
                link(dve.tensor_reduce(lowest[:, :], real, AX.X, ALU.min))
                link(dve.tensor_scalar(bad[:, 1:2], lowest[:, :], 0.0, None, ALU.is_lt))
                link(dve.scalar_tensor_tensor(reach, real, float(NOWHERE // 2), real, ALU.is_lt, ALU.mult))
                link(dve.tensor_reduce(lowest[:, :], reach, AX.X, ALU.max))
                link(dve.tensor_scalar(bad[:, 2:3], lowest[:, :], float(WINDOW), None, ALU.is_ge))
                link(dve.tensor_reduce(lowest[:, :], bad[:, :], AX.X, ALU.max))
                dve.tensor_copy(bad[:, 3:4], lowest[:, :]).then_inc(bad_ready, 1)
                dve.wait_ge(bad_turned, 1)
                link(dve.tensor_copy(bad_row[:, :], ps_b[0:1, 0:P]))
                link(dve.tensor_reduce(bad_row[:, 0:1], bad_row[:, :], AX.X, ALU.max))
                ends_of_parts = range(PART * IG, min(G, -(-E // GROUP) + 2), PART * IG)
                if ends_of_parts:
                    a, b = ends_of_parts[0], ends_of_parts[-1] + 1
                    link(dve.tensor_tensor(bad_row[:, 1:1 + len(ends_of_parts)], win_f[:, a:b:PART * IG],
                                           win_f[:, a - 2:b - 2:PART * IG], ALU.is_equal))
                    link(dve.tensor_reduce(bad_row[:, 0:1], bad_row[:, 0:1 + len(ends_of_parts)], AX.X, ALU.max))
                dve.tensor_copy(general[:, :], bad_row[:, 0:1])
                dve.wait_ge(w_loaded, 15 * 16)
                link(dve.tensor_copy(attn_whole[:, :], attn_sb[:, :]))
                link(dve.tensor_scalar(attn_sb[:, :], attn_sb[:, :], 1.0 - SLOPE, None, ALU.mult))
                for first in (0, ROW):
                    link(dve.tensor_tensor(linear[:, :], w_node[:, first:first + HID], attn_whole[0:F + 1, :], ALU.mult))
                    link(dve.tensor_scalar(linear[:, :], linear[:, :], SLOPE, None, ALU.mult))
                    link(dve.tensor_reduce(w_node[:, first + HID:first + ROW],
                                           linear[:, :].rearrange("p (h f) -> p h f", h=H), AX.X, ALU.add))
                dve.wait_ge(w_turned, 1)
                dve.tensor_copy(wl_in_t[:, 0:HID], ps_w[0:F, 0, 0:HID])
                dve.tensor_copy(wr_in_t[:, 0:HID], ps_w[0:F, 1, 0:HID])
                dve.tensor_copy(w_out_t[:, 0:F], ps_w[0:HID, 2, 0:F])
                dve.tensor_copy(w_out_t[:, F:HID], ps_w[0:HID, 3, 0:F])

            @block.tensor
            def _(pe):
                pe.wait_ge(rows_ready, 1)
                for which in range(2):
                    if which:
                        pe.wait_ge(turned_used, 1)
                    for c in range(K):
                        for k in range(K):
                            t = pe.transpose(ps_t[:, c * K + k, 0:J],
                                             rows_f[0:J, which, c * GROUP + k:(c + 1) * GROUP:K], ident[0:J, 0:J])
                    t.then_inc(turned, 1)
                pe.wait_ge(w_loaded, 15 * 16)
                pe.transpose(ps_w[0:F, 0, 0:HID], w_rows[0:HID, 0, 0:F], ident[0:HID, 0:HID])
                pe.transpose(ps_w[0:F, 1, 0:HID], w_rows[0:HID, 1, 0:F], ident[0:HID, 0:HID])
                pe.transpose(ps_w[0:HID, 2, 0:F], w_rows[0:F, 2, :], ident[0:F, 0:F])
                pe.transpose(ps_w[0:HID, 3, 0:F], w_rows[0:F, 3, :], ident[0:F, 0:F]).then_inc(w_turned, 1)
                pe.wait_ge(win_ready, 1)
                pe.matmul(ps_b[:, 0:G], ones[0:1, :], win_f[0:1, :], start=True, stop=True).then_inc(win_spread, 1)
                pe.wait_ge(bad_ready, 1)
                pe.transpose(ps_b[0:1, 0:P], bad[:, 3:4], ident[:, :]).then_inc(bad_turned, 1)

        def segment_sum_pass(tag, table_dram, table):
            with ExitStack() as ctx:
                ps = [ctx.enter_context(nc.psum_tensor(f"{tag}_ps{i}", [F, SG, WINDOW], F32)) for i in range(2)]
                sem = lambda n: new_sem(ctx, f"{tag}_{n}")
                idx_staged = [sem(f"idx_staged{s}") for s in range(SLOTS)]
                gathered = by_slot[tag]
                onehot_ready, opened = sem("onehot_ready"), sem("opened")
                summed = [sem(f"summed{s}") for s in range(SLOTS)]
                added = [sem(f"added{i}") for i in range(2)]
                block = ctx.enter_context(nc.Block())

                @block.scalar
                def _(act):
                    def iteration(it, first):
                        for s in range(SLOTS):
                            if not first:
                                act.wait_ge(gathered[s], it * (16 * ST))
                            act.activation(idx_buf[:, s, :],
                                           src_idx[:, bass.ds(it * IG + s * SG, SG), :].rearrange("p g k -> p (g k)"),
                                           ACT.Copy).then_inc(idx_staged[s], 1)
                    iterations(act, IT, iteration)

                @block.gpsimd
                def _(pool):
                    def iteration(it, first):
                        for s in range(SLOTS):
                            pool.wait_ge(idx_staged[s], it + 1)
                            if not first:
                                pool.wait_ge(summed[s], it)
                            pool.sem_inc(opened, 1)
                            for t in range(ST):
                                pool.indirect_dma_start(
                                    out=gath[:, s, t, 0:F], out_offset=None, in_=table_dram,
                                    in_offset=bass.IndirectOffsetOnAxis(ap=idx_buf[:, s, t:t + 1], axis=0),
                                ).then_inc(gathered[s], 16)
                    iterations(pool, IT, iteration)

                @block.tensor
                def _(pe):
                    def iteration(it, first):
                        for s in range(SLOTS):
                            par = s % 2
                            pe.wait_ge(onehot_ready, it * SLOTS + s + 1)
                            pe.wait_ge(gathered[s], it * (16 * ST) + 16 * ST)
                            if s >= 2 or not first:
                                pe.wait_ge(added[par], it * IG // 2 + s // 2 * SG)
                            for g in range(SG):
                                for k in range(K):
                                    m = pe.matmul(ps[par][:, g, :], gath[:, s, g * K + k, 0:F],
                                                  onehot[:, par, g * K + k, :], start=(k == 0), stop=(k == K - 1))
                            m.then_inc(summed[s], 1)
                    iterations(pe, IT, iteration)

                @block.vector
                def _(dve):
                    def make_onehot(par, first_group):
                        dve.tensor_tensor(
                            onehot[:, par, :, :], wide(iota[:, :], 1, [P, ST, WINDOW]),
                            wide(dst_rel[:, bass.ds(first_group, SG), :].rearrange("p g k -> p (g k)"), 2, [P, ST, WINDOW]),
                            ALU.is_equal).then_inc(onehot_ready, 1)

                    make_onehot(0, 0)
                    def iteration(it, first):
                        _, starts = nc.values_load_multi_w_load_instructions(
                            win[0:1, bass.ds(it * IG, IG)], engines=DVE_ENGINE, min_val=0, max_val=N,
                            skip_runtime_bounds_check_because=CLAMPED)
                        for s in range(SLOTS):
                            par = s % 2
                            if s or not first:
                                dve.wait_ge(summed[(s - 1) % SLOTS], it + (1 if s else 0))
                            make_onehot(1 - par, it * IG + (s + 1) * SG)
                            dve.wait_ge(summed[s], it + 1)
                            for g in range(SG):
                                if g or s:
                                    prev_par = par if g else 1 - par
                                    prev = s // 2 * SG + g if g else (s - 1) // 2 * SG + SG
                                    dve.wait_ge(added[prev_par], it * (IG // 2) + prev)
                                else:
                                    if not first:
                                        dve.wait_ge(added[1], it * (IG // 2))
                                at = table[0:F, bass.ds(starts[s * SG + g], WINDOW)]
                                dve.tensor_tensor(at, at, ps[par][:, g, :], ALU.add).then_inc(added[par], 1)
                    iterations(dve, IT, iteration)

        NS = IT * SLOTS
        general_e = e_tab[:, BEFORE:BEFORE + G, :, :]
        NB = NK
        SLOT = SG * GROUP
        nc_general = {"min_val": 0, "max_val": 1}

        def only_if_general(engine):
            return engine.If(engine.value_load(general[0:1, 0:1], **nc_general) != 0)

        def done(engine, instruction, sem, count):
            instruction.then_inc(sem, 1)
            engine.wait_ge(sem, count)

        def general_sum(tag, rows, table, slots, fill):
            with ExitStack() as ctx:
                rel = sb(f"{tag}_rel", [P, ST], F32, ctx)
                ps = ctx.enter_context(nc.psum_tensor(f"{tag}_ps", [rows, WINDOW], F32))
                sem = lambda n: new_sem(ctx, f"{tag}_{n}")
                zeroed, begun, dst_in, asked, onehot_ready, summed, added, stepped = map(sem, (
                    "zeroed", "begun", "dst_in", "asked", "onehot_ready", "summed", "added", "stepped"))
                programs = fill(ctx, asked)
                block = ctx.enter_context(nc.Block())

                def over(engine, body):
                    with only_if_general(engine):
                        with engine.Fori(0, slots // SLOT) as n:
                            body(n, SLOT)
                        if slots % SLOT:
                            body(slots // SLOT, slots % SLOT)

                @block.sync
                def _(sp):
                    def body(n, left):
                        sp.wait_ge(asked, n + 1)
                        sp.dma_start(rel[:, :], dcol_dram[:, bass.ds(n * ST, ST)]).then_inc(dst_in, 16)
                        programs["sync"](sp, n, left)
                    over(sp, body)

                @block.gpsimd
                def _(pool):
                    def body(n, left):
                        programs["gpsimd"](pool, n)
                    over(pool, body)

                @block.scalar
                def _(act):
                    def body(n, left):
                        programs["scalar"](act, n)
                    if "scalar" in programs:
                        over(act, body)

                @block.tensor
                def _(pe):
                    def body(n, left):
                        pe.wait_ge(programs["filled"], (n + 1) * programs["signals"])
                        pe.sem_inc(begun, 1)
                        with pe.Fori(0, NB) as b:
                            pe.wait_ge(onehot_ready, n * NB + b + 1)
                            for t in range(ST):
                                m = pe.matmul(ps[:, :], gath[:, 0, t, 0:rows], onehot[:, 0, t, :],
                                              start=(t == 0), stop=(t == ST - 1))
                            m.then_inc(summed, 1)
                    over(pe, body)

                @block.vector
                def _(dve):
                    with only_if_general(dve):
                        done(dve, dve.memset(table[0:rows, :], 0.0), zeroed, 1)

                    def body(n, left):
                        programs["vector"](dve, n)
                        dve.wait_ge(dst_in, (n + 1) * 16)
                        dve.sem_inc(begun, 1)
                        with dve.Fori(0, NB) as b:
                            step = n * NB + b + 1
                            dve.tensor_tensor(onehot[:, 0, :, :], wide(iota[:, :], 1, [P, ST, WINDOW]),
                                              wide(rel[:, :], 2, [P, ST, WINDOW]), ALU.is_equal)\
                               .then_inc(onehot_ready, 1)
                            dve.wait_ge(summed, step)
                            at = table[0:rows, bass.ds(b * WINDOW, WINDOW)]
                            done(dve, dve.tensor_tensor(at, at, ps[:, :], ALU.add), added, step)
                            done(dve, dve.tensor_scalar(rel[:, :], rel[:, :], float(WINDOW), None, ALU.subtract),
                                 stepped, step)
                    over(dve, body)

        def slot_columns(table, n):
            return table[:, bass.ds(n * SG, SG), :].rearrange("p g k -> p (g k)")

        def gathering(tag, table_dram, width):
            gathered = alone[tag]

            def fill(ctx, asked):
                opened = new_sem(ctx, "general_opened")

                def on_vector(dve, n):
                    dve.tensor_copy(idx_buf[:, 0, :], slot_columns(src_idx, n)).then_inc(asked, 1)

                def on_gpsimd(pool, n):
                    pool.wait_ge(asked, n + 1)
                    pool.sem_inc(opened, 1)
                    for t in range(ST):
                        pool.indirect_dma_start(
                            out=gath[:, 0, t, 0:width], out_offset=None, in_=table_dram,
                            in_offset=bass.IndirectOffsetOnAxis(ap=idx_buf[:, 0, t:t + 1], axis=0),
                        ).then_inc(gathered, 16)

                return {"vector": on_vector, "gpsimd": on_gpsimd, "sync": lambda sp, n, left: None,
                        "filled": gathered, "signals": 16 * ST}
            return fill

        def general_scores():
            gathered = alone["scores"]
            with ExitStack() as ctx:
                near = sb("general_dst", [P, ST], F32, ctx)
                sem = lambda n: new_sem(ctx, f"ge_{n}")
                asked, dst_in, indices, opened, link_sem, scored, stored = map(sem, (
                    "asked", "dst_in", "indices", "opened", "link", "scored", "stored"))
                block = ctx.enter_context(nc.Block())

                @block.sync
                def _(sp):
                    with only_if_general(sp):
                        with sp.Fori(0, NS) as n:
                            sp.wait_ge(asked, n + 1)
                            sp.dma_start(near[:, :], dcol_dram[:, bass.ds(n * ST, ST)]).then_inc(dst_in, 16)
                        sp.wait_ge(scored, 1)
                        sp.dma_start(e_dram.rearrange("(g p k) h -> p g (k h)", p=P, k=K),
                                     general_e.rearrange("p g k h -> p g (k h)")).then_inc(stored, 16)
                        sp.wait_ge(stored, 16)

                @block.gpsimd
                def _(pool):
                    with only_if_general(pool):
                        with pool.Fori(0, NS) as n:
                            pool.wait_ge(indices, n + 1)
                            pool.sem_inc(opened, 1)
                            for end, table in enumerate((fs_dram, fd_dram)):
                                for t in range(ST):
                                    pool.indirect_dma_start(
                                        out=gath[:, end, t, 0:table.shape[1]], out_offset=None, in_=table,
                                        in_offset=bass.IndirectOffsetOnAxis(ap=idx_buf[:, end, t:t + 1], axis=0),
                                    ).then_inc(gathered, 16)

                @block.vector
                def _(dve):
                    link = Link(dve, link_sem)
                    with only_if_general(dve):
                        with dve.Fori(0, NS) as n:
                            link.iteration(n, 7, 0)
                            dve.tensor_copy(idx_buf[:, 0, :], slot_columns(src_idx, n)).then_inc(asked, 1)
                            dve.wait_ge(dst_in, n * 16 + 16)
                            link(dve.tensor_scalar(near[:, :], near[:, :], float(N), None, ALU.min))
                            link(dve.tensor_copy(idx_buf[:, 1, :], near[:, :]))
                            dve.wait_ge(asked, n + 1)
                            dve.tensor_copy(near[:, :], near[:, :]).then_inc(indices, 1)
                            dve.wait_ge(gathered, (n + 1) * (2 * 16 * ST))
                            en, ev = gath[:, 0, :, 0:HID], gath[:, 1, :, 0:HID]
                            link(dve.tensor_tensor(ev, en, ev, ALU.add))
                            link(dve.tensor_scalar(gath[:, 2, :, 0:HID], ev, SLOPE, None, ALU.mult))
                            link(dve.tensor_tensor(ev, ev, gath[:, 2, :, 0:HID], ALU.max))
                            link(dve.tensor_tensor(ev, ev, wide(attn_whole[:, :], 1, [P, ST, HID]), ALU.mult))
                            link(dve.tensor_reduce(
                                general_e[:, bass.ds(n * SG, SG), :, :].rearrange("p g k h -> p (g k) h"),
                                ev.rearrange("p t (h f) -> p t h f", h=H), AX.X, ALU.add))
                        dve.memset(near[:, 0:1], 0.0).then_inc(scored, 1)

        def general_softmax():
            with ExitStack() as ctx:
                number = sb("general_number", [P, 1], F32, ctx)
                first = sb("general_first", [P, 1], F32, ctx)
                found = sb("general_found", [P, H], F32, ctx)
                stats = sb("general_stats", [P, NB, 2 * H], F32, ctx)
                e_all = scratch[:, 0:H * LONG].rearrange("p (q h) -> p h q", h=H)
                dst_all = scratch[:, H * LONG:(H + 1) * LONG]
                outside = scratch[:, (H + 1) * LONG:(H + 2) * LONG]
                val = scratch[:, (H + 2) * LONG:(2 * H + 2) * LONG].rearrange("p (h q) -> p h q", h=H)
                sem = lambda n: new_sem(ctx, f"gs_{n}")
                number_in, link_sem, stats_ready, stored, begun = map(
                    sem, ("number_in", "link", "stats_ready", "stored", "begun"))
                passes = [{n: sem(f"{n}{i}") for n in ("asked", "rows_in", "outside", "val", "centred", "exp",
                                                       "found", "kept", "stepped")} for i in range(2)]
                block = ctx.enter_context(nc.Block())

                @block.sync
                def _(sp):
                    with only_if_general(sp):
                        for s in passes:
                            with sp.Fori(0, J) as q:
                                sp.wait_ge(s["asked"], q + 1)
                                sp.dma_start(scratch[:, 0:H * LONG],
                                             e_dram.rearrange("(j q) h -> j (q h)", q=LONG)[bass.ds(q, 1), :]
                                             .to_broadcast([P, H * LONG])).then_inc(s["rows_in"], 16)
                                sp.dma_start(dst_all, drow_dram[bass.ds(q, 1), :].to_broadcast([P, LONG]))\
                                  .then_inc(s["rows_in"], 16)
                        sp.wait_ge(stats_ready, 1)
                        sp.dma_start(nd_dram.rearrange("(b p) c -> p b c", p=P), stats[:, :, :]).then_inc(stored, 16)
                        sp.wait_ge(stored, 16)

                @block.scalar
                def _(act):
                    with only_if_general(act):
                        s = passes[1]
                        with act.Fori(0, J) as q:
                            with act.Fori(0, NB) as b:
                                act.wait_ge(s["centred"], q * NB + b + 1)
                                act.activation(val, val, ACT.Exp).then_inc(s["exp"], 1)

                @block.gpsimd
                def _(pool):
                    with only_if_general(pool):
                        pool.iota(idx_buf[:, 0, 0:1], [[0, 1]], base=0, channel_multiplier=1).then_inc(number_in, 1)

                @block.vector
                def _(dve):
                    link = Link(dve, link_sem)
                    with only_if_general(dve):
                        dve.wait_ge(number_in, 1)
                        link(dve.tensor_copy(first[:, :], idx_buf[:, 0, 0:1]))
                        link(dve.memset(stats[:, :, 0:H], -BIG / 16))
                        link(dve.memset(stats[:, :, H:2 * H], 0.0))
                        for which, s in enumerate(passes):
                            with dve.Fori(0, J) as q:
                                dve.tensor_copy(number[:, :], first[:, :]).then_inc(s["asked"], 1)
                                dve.wait_ge(s["asked"], q + 1)
                                dve.wait_ge(s["rows_in"], q * 32 + 32)
                                dve.sem_inc(begun, 1)
                                with dve.Fori(0, NB) as b:
                                    step = q * NB + b + 1
                                    done(dve, dve.tensor_scalar(outside, dst_all, number[:, 0:1], -BIG,
                                                                ALU.not_equal, ALU.mult), s["outside"], step)
                                    done(dve, dve.tensor_tensor(val, e_all, wide(outside, 1, [P, H, LONG]), ALU.add),
                                         s["val"], step)
                                    tops = stats[:, bass.ds(b, 1), 0:H].rearrange("p b h -> p (b h)")
                                    sums = stats[:, bass.ds(b, 1), H:2 * H].rearrange("p b h -> p (b h)")
                                    if which:
                                        dve.tensor_tensor(val, val, wide(tops, 2, [P, H, LONG]), ALU.subtract)\
                                           .then_inc(s["centred"], 1)
                                        dve.wait_ge(s["exp"], step)
                                    op, kept = (ALU.add, sums) if which else (ALU.max, tops)
                                    done(dve, dve.tensor_reduce(found[:, :], val, AX.X, op), s["found"], step)
                                    done(dve, dve.tensor_tensor(kept, kept, found[:, :], op), s["kept"], step)
                                    done(dve, dve.tensor_scalar(number[:, :], number[:, :], float(P), None, ALU.add),
                                         s["stepped"], step)
                        sums = stats[:, :, H:2 * H]
                        link(dve.tensor_scalar(sums, sums, 1e-9, None, ALU.max))
                        link(dve.reciprocal(sums, sums))
                        dve.memset(number[:, :], 0.0).then_inc(stats_ready, 1)

        def messages():
            gathered = alone["messages"]

            def fill(ctx, asked):
                near = sb("general_near", [P, ST], F32, ctx)
                exps = sb("general_exps", [P, ST, H], F32, ctx)
                weight = sb("general_weight", [P, ST, H], F32, ctx)
                sem = lambda n: new_sem(ctx, f"gm_{n}")
                near_in, indices, opened, filled, r_in, link_sem, less, exp_done, centred, msg_exp = map(sem, (
                    "near_in", "indices", "opened", "filled", "r_in", "link", "less", "exp_done", "centred",
                    "msg_exp"))
                r_view = edge_attr.rearrange("e h f -> e (h f)")
                en, r = gath[:, 0, :, 0:HID], gath[:, 2, :, 0:HID]
                tops, recips = gath[:, 1, :, 0:H], gath[:, 1, :, H:2 * H]

                def on_sync(sp, n, left):
                    sp.dma_start(near[:, :], dcol_dram[:, bass.ds(n * ST, ST)]).then_inc(near_in, 16)
                    for g in range(SG):
                        parts = min(P, max(0, left - g * GROUP) // K)
                        if parts:
                            sp.dma_start(gath[0:parts, 2, g * K:(g + 1) * K, 0:HID],
                                         r_view[bass.ds((n * SG + g) * GROUP, parts * K), :]
                                         .rearrange("(p k) f -> p k f", k=K)).then_inc(r_in, 16)
                        else:
                            sp.sem_inc(r_in, 16)

                def on_gpsimd(pool, n):
                    pool.wait_ge(indices, n + 1)
                    pool.sem_inc(opened, 1)
                    for end, (table, width) in enumerate(((fs_dram, fs_dram.shape[1]), (nd_dram, 2 * H))):
                        for t in range(ST):
                            pool.indirect_dma_start(
                                out=gath[:, end, t, 0:width], out_offset=None, in_=table,
                                in_offset=bass.IndirectOffsetOnAxis(ap=idx_buf[:, end, t:t + 1], axis=0),
                            ).then_inc(gathered, 16)

                def on_scalar(act, n):
                    act.wait_ge(less, n + 1)
                    act.activation(exps[:, :, :], exps[:, :, :], ACT.Exp).then_inc(exp_done, 1)
                    act.wait_ge(centred, n + 1)
                    act.activation(en, en, ACT.Exp).then_inc(msg_exp, 1)

                def on_vector(dve, n):
                    link = Link(dve, link_sem)
                    link.iteration(n, 9, 0)
                    heads = lambda ap: ap.rearrange("p t (h f) -> p t h f", h=H)
                    over = lambda ap: wide(ap, 3, [P, ST, H, F])
                    dve.tensor_copy(idx_buf[:, 0, :], slot_columns(src_idx, n)).then_inc(asked, 1)
                    dve.wait_ge(near_in, n * 16 + 16)
                    link(dve.tensor_scalar(near[:, :], near[:, :], float(N), None, ALU.min))
                    link(dve.tensor_copy(idx_buf[:, 1, :], near[:, :]))
                    dve.wait_ge(asked, n + 1)
                    dve.tensor_copy(near[:, :], near[:, :]).then_inc(indices, 1)
                    dve.wait_ge(gathered, (n + 1) * (2 * 16 * ST))
                    dve.wait_ge(r_in, (n + 1) * (16 * SG))
                    scores = general_e[:, bass.ds(n * SG, SG), :, :].rearrange("p g k h -> p (g k) h")
                    link(dve.tensor_tensor(exps[:, :, :], scores, tops, ALU.subtract))
                    dve.tensor_scalar(exps[:, :, :], exps[:, :, :], 0.0, None, ALU.min).then_inc(less, 1)
                    link(dve.tensor_tensor(en, en, r, ALU.mult))
                    link(dve.tensor_reduce(weight[:, :, :], heads(en), AX.X, ALU.max))
                    link(dve.tensor_tensor(heads(en), heads(en), over(weight[:, :, :]), ALU.subtract))
                    dve.wait_ge(exp_done, n + 1)
                    link(dve.tensor_tensor(weight[:, :, :], exps[:, :, :], recips, ALU.mult))
                    dve.tensor_tensor(heads(en), heads(en), over(weight[:, :, :]), ALU.mult).then_inc(centred, 1)
                    dve.wait_ge(msg_exp, n + 1)
                    link(dve.tensor_reduce(weight[:, :, :], heads(en), AX.X, ALU.add))
                    link(dve.reciprocal(weight[:, :, :], weight[:, :, :]))
                    dve.tensor_tensor(heads(en), heads(en), over(weight[:, :, :]), ALU.mult).then_inc(filled, 1)

                return {"vector": on_vector, "gpsimd": on_gpsimd, "sync": on_sync, "scalar": on_scalar,
                        "filled": filled, "signals": 1}
            return fill

        segment_sum_pass("sum_x", x, table_a)
        general_sum("all_x", F, table_a, E, gathering("all_x", x, F))

        with ExitStack() as ctx:
            xt = sb("xt", [F, 2, K, P], F32, ctx)
            stage = sb("stage", [P, 2, K, F], F32, ctx)
            hid = sb("hid", [HID, 2, K, P], F32, ctx)
            y_sb = scratch[:, 0:NK * F].rearrange("p (c k f) -> p c k f", k=K, f=F)
            ps_x = [ctx.enter_context(nc.psum_tensor(f"ps_x{i}", [F, K, P], F32)) for i in range(2)]
            ps_h = [ctx.enter_context(nc.psum_tensor(f"ps_h{i}", [P, K, P], F32)) for i in range(2)]
            ps_y = [ctx.enter_context(nc.psum_tensor(f"ps_y{i}", [P, K, HID], F32)) for i in range(2)]
            sem = lambda n: new_sem(ctx, f"n0_{n}")
            staged, x_turned, x_copied, h_summed, h_ready, y_summed, y_used, y_stored = map(
                sem, ("staged", "x_turned", "x_copied", "h_summed", "h_ready", "y_summed", "y_used", "y_stored"))
            block = ctx.enter_context(nc.Block())

            @block.tensor
            def _(pe):
                def step(c, par, lo, hi):
                    if inside(NCH, lo, hi, 0):
                        pe.wait_ge(staged, c + 1)
                        if lo >= 2:
                            pe.wait_ge(x_copied, c - 1)
                        for k in range(K):
                            t = pe.transpose(ps_x[par][:, k, :], stage[:, par, k, :], ident[:, :])
                        t.then_inc(x_turned, 1)
                    if inside(NCH, lo, hi, 1):
                        pe.wait_ge(x_copied, c)
                        if lo >= 3:
                            pe.wait_ge(h_ready, c - 2)
                        q = 1 - par
                        pe.matmul(ps_h[q][:, :, :], wl_in_t[:, :],
                                  table_a[0:F, bass.ds((c - 1) * GROUP, GROUP)].rearrange("f (p k) -> f k p", k=K),
                                  start=True, stop=False)
                        pe.matmul(ps_h[q][:, :, :], wr_in_t[:, :], xt[:, q, :, :], start=False, stop=True)\
                          .then_inc(h_summed, 1)
                    if inside(NCH, lo, hi, 2):
                        pe.wait_ge(h_ready, c - 1)
                        if lo >= 4:
                            pe.wait_ge(y_used, c - 3)
                        for k in range(K):
                            m = pe.matmul(ps_y[par][:, k, :], hid[:, par, k, :], w_out_t[:, :], start=True, stop=True)
                        m.then_inc(y_summed, 1)
                skewed(pe, NCH, 2, step)

            @block.scalar
            def _(act):
                def step(c, par, lo, hi):
                    if inside(NCH, lo, hi, 0):
                        act.wait_ge(x_turned, c + 1)
                        if lo >= 2:
                            act.wait_ge(h_summed, c - 1)
                        act.activation(xt[:, par, :, :], ps_x[par][:, :, :], ACT.Copy).then_inc(x_copied, 1)
                    if inside(NCH, lo, hi, 1):
                        act.wait_ge(h_summed, c)
                        if lo >= 3:
                            act.wait_ge(y_summed, c - 2)
                        act.activation(hid[:, 1 - par, :, :], ps_h[1 - par][0:HID, :, :], ACT.Relu, bias=b_in[:, 0:1])\
                           .then_inc(h_ready, 1)
                skewed(act, NCH, 1, step)

            @block.vector
            def _(dve):
                def step(c, par, lo, hi):
                    if inside(NCH, lo, hi, 0):
                        if lo >= 2:
                            dve.wait_ge(x_turned, c - 1)
                        dve.tensor_copy(stage[:, par, :, :], nodes[:, bass.ds(c, 1), :, :]
                                        .rearrange("p c k f -> p (c k) f")).then_inc(staged, 1)
                    if inside(NCH, lo, hi, 2):
                        dve.wait_ge(y_summed, c - 1)
                        dve.tensor_copy(y_sb[:, bass.ds(c - 2, 1), :, :].rearrange("p c k f -> p (c k) f"),
                                        ps_y[par][:, :, 0:F])
                        dve.tensor_copy(rest[:, bass.ds(c - 2, 1), :, :].rearrange("p c k f -> p (c k) f"),
                                        ps_y[par][:, :, F:HID]).then_inc(y_used, 1)
                skewed(dve, NCH, 2, step)

            @block.sync
            def _(sp):
                sp.wait_ge(y_used, NCH)
                sp.dma_start(y_dram.rearrange("(c p k) f -> p c (k f)", p=P, k=K),
                             y_sb.rearrange("p c k f -> p c (k f)")).then_inc(y_stored, 16)
                sp.wait_ge(y_stored, 16)

        with ExitStack() as ctx:
            block = ctx.enter_context(nc.Block())

            @block.vector
            def _(dve):
                dve.memset(table_b[0:F, :], 0.0)

            @block.gpsimd
            def _(pool):
                pool.memset(table_a[0:HID, :], 0.0)

        segment_sum_pass("sum_y", y_dram, table_b)
        general_sum("all_y", F, table_b, E, gathering("all_y", y_dram, F))
        reset_semaphores()

        def layer_norm(dve, act_sqrt, sqrt_done, link, v, work, mean, var, result):
            link(dve.tensor_reduce(mean[:, :], v, AX.X, ALU.add))
            link(dve.tensor_scalar(mean[:, :], mean[:, :], 1.0 / F, None, ALU.mult))
            link(dve.tensor_tensor(v, v, wide(mean[:, :], 2, [P, NK, F]), ALU.subtract))
            link(dve.tensor_tensor(work, v, v, ALU.mult))
            link(dve.tensor_reduce(var[:, :], work, AX.X, ALU.add))
            dve.tensor_scalar(var[:, :], var[:, :], 1.0 / F, EPS, ALU.mult, ALU.add).then_inc(act_sqrt, 1)
            dve.wait_ge(sqrt_done, 1)
            link(dve.reciprocal(var[:, :], var[:, :]))
            link(dve.tensor_tensor(result, v, wide(var[:, :], 2, [P, NK, F]), ALU.mult))

        with ExitStack() as ctx:
            mean = sb("mean", [P, NK], F32, ctx)
            var = sb("var", [P, NK], F32, ctx)
            xt = sb("x1t", [F + 1, 2, K, P], F32, ctx)
            stage = sb("stage1", [P, 2, K, F], F32, ctx)
            fsd = sb("fsd", [P, 2, 2, K, ROW], F32, ctx)
            bl_out_b = sb("bl_out_b2", [P, F], F32, ctx)
            work = scratch[:, NCH * GROUP:NCH * GROUP + NK * F].rearrange("p (a f) -> p a f", f=F)
            sem = lambda n: new_sem(ctx, f"n1_{n}")
            (staged, bias_loaded, turned, link_sem, var_ready, sqrt_done, x1_ready, x_turned, x_copied, f_summed,
             f_copied, r_copied) = map(sem, (
                "staged", "bias_loaded", "turned", "link", "var_ready", "sqrt_done", "x1_ready", "x_turned",
                "x_copied", "f_summed", "f_copied", "r_copied"))
            stored = [sem(f"stored{i}") for i in range(2)]
            flat_rest = rest[:, :, :, :].rearrange("p c k f -> p (c k) f")

            with ExitStack() as part:
                ps = part.enter_context(nc.psum_tensor("ps_agg", [P, NK, F], F32))
                block = part.enter_context(nc.Block())

                @block.sync
                def _(sp):
                    sp.dma_start(bl_out_b[:, :], bl_out.rearrange("(a f) -> a f", a=1).to_broadcast([P, F]))\
                      .then_inc(bias_loaded, 16)
                    sp.wait_ge(bias_loaded, 16)

                @block.tensor
                def _(pe):
                    for c in range(NCH):
                        for k in range(K):
                            t = pe.transpose(ps[:, c * K + k, :], table_b[0:F, c * GROUP + k:(c + 1) * GROUP:K],
                                             ident[0:F, 0:F])
                    t.then_inc(turned, 1)

                @block.scalar
                def _(act):
                    act.wait_ge(var_ready, 1)
                    act.activation(var[:, :], var[:, :], ACT.Sqrt).then_inc(sqrt_done, 1)

                @block.vector
                def _(dve):
                    link = Link(dve, link_sem)
                    link(dve.tensor_tensor(flat_nodes, flat_nodes, flat_rest, ALU.add))
                    dve.wait_ge(bias_loaded, 16)
                    link(dve.tensor_tensor(flat_nodes, flat_nodes, wide(bl_out_b[:, :], 1, [P, NK, F]), ALU.add))
                    dve.wait_ge(turned, 1)
                    link(dve.tensor_tensor(flat_nodes, flat_nodes, ps[:, :, :], ALU.add))
                    layer_norm(dve, var_ready, sqrt_done, link, flat_nodes, work, mean, var, flat_nodes)
                    dve.memset(xt[F:F + 1, :, :, :], 1.0)

            ps_x = [ctx.enter_context(nc.psum_tensor(f"ps_x1{i}", [F, K, P], F32)) for i in range(2)]
            ps_f = [ctx.enter_context(nc.psum_tensor(f"ps_f{i}", [P, K, 256], F32)) for i in range(2)]
            block = ctx.enter_context(nc.Block())
            WN = 2 * ROW + F

            @block.tensor
            def _(pe):
                def step(c, par, lo, hi):
                    if inside(NCH, lo, hi, 0):
                        pe.wait_ge(staged, c + 1)
                        if lo >= 2:
                            pe.wait_ge(x_copied, c - 1)
                        for k in range(K):
                            t = pe.transpose(ps_x[par][:, k, :], stage[:, par, k, :], ident[:, :])
                        t.then_inc(x_turned, 1)
                    if inside(NCH, lo, hi, 1):
                        q = 1 - par
                        pe.wait_ge(x_copied, c)
                        if lo >= 3:
                            pe.wait_ge(f_copied, c - 2)
                            pe.wait_ge(r_copied, c - 2)
                        for k in range(K):
                            m = pe.matmul(ps_f[q][:, k, 0:WN], xt[:, q, k, :], w_node[:, :], start=True, stop=True)
                        m.then_inc(f_summed, 1)
                skewed(pe, NCH, 1, step)

            @block.scalar
            def _(act):
                def step(c, par, lo, hi):
                    if inside(NCH, lo, hi, 0):
                        act.wait_ge(x_turned, c + 1)
                        if lo >= 2:
                            act.wait_ge(f_summed, c - 1)
                        act.activation(xt[0:F, par, :, :], ps_x[par][:, :, :], ACT.Copy).then_inc(x_copied, 1)
                    if inside(NCH, lo, hi, 1):
                        q = 1 - par
                        act.wait_ge(f_summed, c)
                        if lo >= 3:
                            act.wait_ge(stored[q], (c - 2 + par) * 16)
                        act.activation(fsd[:, q, 0, :, :], ps_f[q][:, :, 0:ROW], ACT.Copy)
                        act.activation(fsd[:, q, 1, :, :], ps_f[q][:, :, ROW:2 * ROW], ACT.Copy).then_inc(f_copied, 1)
                skewed(act, NCH, 1, step)

            @block.vector
            def _(dve):
                def step(c, par, lo, hi):
                    if inside(NCH, lo, hi, 0):
                        if lo >= 2:
                            dve.wait_ge(x_turned, c - 1)
                        dve.tensor_copy(stage[:, par, :, :], nodes[:, bass.ds(c, 1), :, :]
                                        .rearrange("p c k f -> p (c k) f")).then_inc(staged, 1)
                    if inside(NCH, lo, hi, 1):
                        dve.wait_ge(f_copied, c)
                        dve.tensor_tensor(rest[:, bass.ds(c - 1, 1), :, :].rearrange("p c k f -> p (c k) f"),
                                          nodes[:, bass.ds(c - 1, 1), :, :].rearrange("p c k f -> p (c k) f"),
                                          ps_f[1 - par][:, :, 2 * ROW:WN], ALU.add).then_inc(r_copied, 1)
                skewed(dve, NCH, 1, step)

            @block.sync
            def _(sp):
                def step(c, par, lo, hi):
                    if inside(NCH, lo, hi, 0):
                        sp.wait_ge(f_copied, c + 1)
                        for which, table in enumerate((fs_dram, fd_dram)):
                            sp.dma_start(table[bass.ds(c * GROUP, GROUP), :].rearrange("(p k) f -> p (k f)", k=K),
                                         fsd[:, par, which, :, :].rearrange("p k f -> p (k f)")).then_inc(stored[par], 16)
                skewed(sp, NCH, 0, step)
                sp.wait_ge(stored[0], (NCH + 1) // 2 * 32)
                sp.wait_ge(stored[1], NCH // 2 * 32)

        LAG = (PART + 1) * SLOTS + 1
        NS = IT * SLOTS
        assert PART * IG + BEFORE <= SROWS and IT > PART + 3
        with ExitStack() as ctx:
            def take(at, *shape):
                size = 1
                for d in shape:
                    size *= d
                piece = scratch[:, at:at + size]
                if len(shape) == 2:
                    piece = piece.rearrange("p (a b) -> p a b", a=shape[0])
                elif len(shape) == 3:
                    piece = piece.rearrange("p (a b c) -> p a b c", a=shape[0], b=shape[1])
                return piece, at + size

            oht, at = take(0, 2, ST, P)
            oh_msg, at = take(at, 2, ST, WINDOW)
            en, at = take(at, SLOTS, ST, ROW)
            r, at = take(at, SLOTS, ST, HID)
            lrelu, at = take(at, ST, HID)
            e_row, at = take(at, GROUP)
            f_row, at = take(at, GROUP)
            back, at = take(at, GROUP)
            cont, at = take(at, GROUP + 1)
            cneg, at = take(at, GROUP + 1)
            isend, at = take(at, GROUP)
            dst_f, at = take(at, GROUP + 1)
            dst_i = dst_f.bitcast(I32)
            attn_in_nodes = nodes[:, :, :, :].rearrange("p c k f -> p (c k f)")[:, 0:G * K * H]
            a_tab = attn_in_nodes.rearrange("p (g k h) -> p g k h", k=K, h=H)
            assert at <= 16400
            fdw = sb("fdw", [WINDOW, SLOTS, SG, ROW], F32, ctx)
            lin = sb("lin", [P, ST, H], F32, ctx)
            top = sb("top", [P, ST * H], F32, ctx)
            weight = sb("weight", [P, SLOTS, ST * H], F32, ctx)
            bias = sb("bias", [P, SLOTS, ST * H], F32, ctx)
            total = sb("total", [P, SLOTS, ST * H], F32, ctx)
            ends = sb("ends", [P, 4], F32, ctx)
            rowd = sb("rowd", [1, 13, P + 2], F32, ctx)
            FIRST, LAST, SAME, JOIN, NEXT, BOTH, BOTHN, NBOTH, NBOTHN, NJOIN, NNEXT, VALUE, STATE = range(13)
            saved = sb("saved", [1, 2, H], F32, ctx)
            cin = sb("cin", [1, P], F32, ctx)
            ps_o = [ctx.enter_context(nc.psum_tensor(f"ps_o{i}", [WINDOW, K, P], F32)) for i in range(2)]
            ps_e = [ctx.enter_context(nc.psum_tensor(f"ps_e{i}", [P, K, P], F32)) for i in range(2)]
            ps_m = [ctx.enter_context(nc.psum_tensor(f"ps_m{i}", [HID, 512], F32)) for i in range(2)]
            ps_s = ctx.enter_context(nc.psum_tensor("ps_s", [P, K, P], F32))
            ps_r = ctx.enter_context(nc.psum_tensor("ps_r", [P, 512], F32))

            def sem(n):
                return new_sem(ctx, f"e_{n}")

            idx_staged = [sem(f"idx_staged{s}") for s in range(SLOTS)]
            gathered = by_slot["scores"]
            fd_loaded = [sem(f"fd_loaded{s}") for s in range(SLOTS)]
            en_stored = [sem(f"en_stored{s}") for s in range(SLOTS)]
            onehot_ready, opened = sem("onehot_ready"), sem("opened")
            turned, copied, spread, spread_used = ([sem(f"{n}{g}") for g in range(SG)] for n in (
                "turned", "copied", "spread", "spread_used"))
            masked, reduced, scored = sem("masked"), sem("reduced"), sem("scored")
            dst_in, masks_made, s_link, e_turned, ends_ready, ends_turned, cin_ready, cin_turned, shifted, \
                exped, a_ready, a_turned, a_copied, s_set, e_staged = map(sem, (
                    "dst_in", "masks_made", "s_link", "e_turned", "ends_ready", "ends_turned", "cin_ready",
                    "cin_turned", "shifted", "exped", "a_ready", "a_turned", "a_copied", "s_set", "e_staged"))
            loaded = [sem(f"loaded{s}") for s in range(SLOTS)]
            (multiplied, top_ready, bias_ready, exp_done, sum_ready, rec_ready, msg_ready, oh_msg_ready, summed,
             added) = map(sem, ("multiplied", "top_ready", "bias_ready", "exp_done", "sum_ready", "rec_ready",
                                "msg_ready", "oh_msg_ready", "summed", "added"))
            block = ctx.enter_context(nc.Block())
            r_view = edge_attr.rearrange("e h f -> e (h f)")

            def walk(engine, before, step, softmax, lag=LAG):
                def is_static(it):
                    return it % PART == 0 or -SLOTS < it * SLOTS - lag < SLOTS

                it = 0
                while it < IT:
                    if is_static(it):
                        before(it)
                        for s in range(SLOTS):
                            if it and it % PART == 0:
                                softmax(it // PART - 1, s)
                            m = it * SLOTS + s
                            step(m, m - lag if m >= lag else None, s)
                        it += 1
                        continue
                    end = it
                    while end < IT and not is_static(end):
                        end += 1
                    with engine.Fori(it, end) as i:
                        before(i, it * SLOTS >= lag)
                        for s in range(SLOTS):
                            m = i * SLOTS + s
                            step(m, m - lag if it * SLOTS >= lag else None, s)
                    it = end
                for piece in range(SLOTS):
                    softmax((IT - 1) // PART, piece)
                n = NS - lag
                loops = (NS - SLOTS - n) // SLOTS
                with engine.Fori(0, loops) as i:
                    before(("tail", i * SLOTS + n))
                    for u in range(SLOTS):
                        step(None, i * SLOTS + (n + u), (n + u) % SLOTS)
                for n in range(n + loops * SLOTS, NS + 3):
                    before(("tail", n))
                    step(None, n, n % SLOTS)

            def exists(n, lag):
                return n is not None and (not isinstance(n, int) or 0 <= n - lag < NS)

            def after(n, least):
                return not isinstance(n, int) or n >= least

            def slot_count(m, s, per):
                if isinstance(m, int):
                    return (m // SLOTS + 1) * per
                return (m - s) * (per // SLOTS) + per

            @block.sync
            def _(sp):
                AHEAD = LAG - 1
                starts = []

                def load_dst(part):
                    first = part * PART * IG * GROUP
                    for h in range(H):
                        rows = slice(h * SROWS, (h + 1) * SROWS)
                        sp.dma_start(dst_i[rows, 0:GROUP], dst_dram[first:first + SROWS * GROUP]
                                     .rearrange("(j q) -> j q", q=GROUP)).then_inc(dst_in, 16)
                        sp.dma_start(dst_i[rows, GROUP:GROUP + 1],
                                     dst_dram[first + GROUP:first + SROWS * GROUP + 1:GROUP]
                                     .rearrange("(j a) -> j a", a=1), allow_slow_non_contiguous=True)\
                          .then_inc(dst_in, 16)

                def before(it, messages=True):
                    if not isinstance(it, tuple):
                        starts[:] = nc.values_load_multi_w_load_instructions(
                            win[0:1, bass.ds(it * IG, IG)], engines=SP_ENGINE, min_val=0, max_val=N,
                            skip_runtime_bounds_check_because=CLAMPED)[1]

                def step(m, n, s):
                    if m is not None:
                        if after(m, SLOTS):
                            sp.wait_ge(spread[SG - 1], m - (SLOTS - 1))
                        for g in range(SG):
                            sp.dma_start(fdw[:, s, g, :], fd_dram[bass.ds(starts[s * SG + g], WINDOW), :])\
                              .then_inc(fd_loaded[s], 16)
                    if exists(n, 0):
                        q = s if m is None else (s - AHEAD) % SLOTS
                        if after(n, SLOTS):
                            sp.wait_ge(summed, n - (SLOTS - 1))
                        sp.wait_ge(en_stored[q], slot_count(n, q, 16))
                        sp.dma_start(en[:, q, :, :].rearrange("p t f -> p (t f)"),
                                     en_dram[bass.ds(n, 1), :, :].rearrange("a p f -> (a p) f"))\
                          .then_inc(loaded[q], 16)
                        for g in range(SG):
                            parts = P
                            if isinstance(n, int):
                                parts = min(P, max(0, E - (n * SG + g) * GROUP) // K)
                            if parts:
                                sp.dma_start(r[0:parts, q, g * K:(g + 1) * K, :].rearrange("p t f -> p (t f)"),
                                             r_view[bass.ds((n * SG + g) * GROUP, parts * K), :]
                                             .rearrange("(p k) f -> p (k f)", k=K)).then_inc(loaded[q], 16)
                    if m is not None:
                        sp.wait_ge(gathered[s], slot_count(m, s, 16 * ST))
                        sp.dma_start(en_dram[bass.ds(m, 1), :, :].rearrange("a p f -> (a p) f"),
                                     gath[:, s, :, :].rearrange("p t f -> p (t f)")).then_inc(en_stored[s], 16)

                def softmax(part, piece):
                    if piece == 0:
                        sp.wait_ge(masks_made, part + 1)
                        if (part + 1) * PART < IT:
                            load_dst(part + 1)
                    if piece == 3 and (part + 1) * PART >= IT:
                        for s in range(SLOTS):
                            sp.wait_ge(en_stored[s], IT * 16)

                sp.wait_ge(s_set, 1)
                load_dst(0)
                walk(sp, before, step, softmax, AHEAD)

            @block.gpsimd
            def _(pool):
                def iteration(it, first):
                    for s in range(SLOTS):
                        pool.wait_ge(idx_staged[s], it + 1)
                        if not first:
                            pool.wait_ge(spread[SG - 1], it * SLOTS + (s - SLOTS + 1))
                            pool.wait_ge(en_stored[s], it * 16)
                        pool.sem_inc(opened, 1)
                        for t in range(ST):
                            pool.indirect_dma_start(
                                out=gath[:, s, t, :], out_offset=None, in_=fs_dram,
                                in_offset=bass.IndirectOffsetOnAxis(ap=idx_buf[:, s, t:t + 1], axis=0),
                            ).then_inc(gathered[s], 16)
                iterations(pool, IT, iteration)

            @block.tensor
            def _(pe):
                def turn(m, par):
                    pe.wait_ge(onehot_ready, m + 1)
                    for g in range(SG):
                        if after(m, 1):
                            pe.wait_ge(copied[g], m)
                        for k in range(K):
                            t = pe.transpose(ps_o[g][:, k, :], onehot[:, par, g * K + k, :], ident[:, :])
                        t.then_inc(turned[g], 1)

                def step(m, n, s):
                    if m is not None:
                        pe.wait_ge(fd_loaded[s], slot_count(m, s, 16 * SG))
                        pe.wait_ge(gathered[s], slot_count(m, s, 16 * ST))
                        for g in range(SG):
                            pe.wait_ge(copied[g], m + 1)
                            if after(m, 1):
                                pe.wait_ge(spread_used[g], m)
                            for k in range(K):
                                pe.matmul(ps_e[g][:, k, 0:ROW], oht[:, s % 2, g * K + k, :], fdw[:, s, g, :],
                                          start=True, stop=False)
                                t = pe.matmul(ps_e[g][:, k, 0:ROW], ident[:, :], gath[:, s, g * K + k, :],
                                              start=False, stop=True)
                            t.then_inc(spread[g], 1)
                        turn(m + 1, (s + 1) % 2)
                    if exists(n, 2):
                        q = (s - 2 - (0 if m is None else LAG)) % SLOTS
                        par = q % 2
                        pe.wait_ge(msg_ready, n - 1)
                        pe.wait_ge(oh_msg_ready, n - 1)
                        if after(n, 4):
                            pe.wait_ge(added, (n - 3) * SG)
                        for g in range(SG):
                            for k in range(K):
                                t = pe.matmul(ps_m[par][:, g * WINDOW:(g + 1) * WINDOW],
                                              en[:, q, g * K + k, 0:HID], oh_msg[:, par, g * K + k, :],
                                              start=(k == 0), stop=(k == K - 1))
                        t.then_inc(summed, 1)

                def softmax(part, piece):
                    def out_and_back(n):
                        pe.wait_ge(ends_ready, part * 5 + 2 + n)
                        pe.transpose(ps_r[0:1, 0:P], ends[:, 2:3], ident[:, :]).then_inc(ends_turned, 1)
                        pe.wait_ge(cin_ready, part * 4 + 1 + n)
                        pe.transpose(ps_r[:, 256:257], cin[0:1, :], ident[0:1, 0:1]).then_inc(cin_turned, 1)

                    if piece == 0:
                        pe.wait_ge(e_staged, part + 1)
                        if part:
                            pe.wait_ge(a_copied, part * H)
                        for k in range(K):
                            t = pe.transpose(ps_s[:, k, :], f_row[:, k * P:(k + 1) * P], ident[:, :])
                        t.then_inc(e_turned, 1)
                        pe.wait_ge(ends_ready, part * 5 + 1)
                        pe.transpose(ps_r[0:1, 0:P], ends[:, 0:1], ident[:, :])
                        pe.transpose(ps_r[0:1, P:2 * P], ends[:, 1:2], ident[:, :]).then_inc(ends_turned, 1)
                    if piece == 1:
                        out_and_back(0)
                        out_and_back(1)
                    if piece == 2:
                        out_and_back(2)
                        out_and_back(3)
                    if piece == 3:
                        pe.wait_ge(a_ready, part + 1)
                        for k in range(K):
                            t = pe.transpose(ps_s[:, k, :], e_row[:, k:GROUP:K], ident[:, :])
                        t.then_inc(a_turned, 1)

                turn(0, 0)
                walk(pe, lambda it, messages=True: None, step, softmax)

            @block.scalar
            def _(act):
                AHEAD = SLOTS - 1

                def stage(m, s):
                    if after(m, SLOTS):
                        act.wait_ge(gathered[s], slot_count(m, s, 16 * ST) - 16 * ST)
                    act.activation(idx_buf[:, s, :], src_idx[:, bass.ds(m * SG, SG), :].rearrange("p g k -> p (g k)"),
                                   ACT.Copy).then_inc(idx_staged[s], 1)

                def copy_turned(m, par):
                    for g in range(SG):
                        act.wait_ge(turned[g], m + 1)
                        if after(m, 2):
                            act.wait_ge(spread[g], m - 1)
                        act.activation(oht[:, par, g * K:(g + 1) * K, :], ps_o[g][:, :, :], ACT.Copy)\
                           .then_inc(copied[g], 1)

                def step(m, n, s):
                    if m is not None:
                        stage(m + AHEAD, (s + AHEAD) % SLOTS)
                        copy_turned(m + 1, (s + 1) % 2)
                    if exists(n, 0):
                        q = s if m is None else (s - LAG) % SLOTS
                        act.wait_ge(bias_ready, n + 1)
                        for i in range(ST * H):
                            rows = en[:, q, i // H, i % H * F:(i % H + 1) * F]
                            e = act.activation(rows, rows, ACT.Exp, bias=bias[:, q, i:i + 1],
                                               scale=weight[:, q, i:i + 1])
                        e.then_inc(exp_done, 1)

                def softmax(part, piece):
                    if piece == 2:
                        act.wait_ge(shifted, part + 1)
                        act.activation(e_row, e_row, ACT.Exp).then_inc(exped, 1)

                for m in range(AHEAD):
                    stage(m, m)
                copy_turned(0, 0)
                walk(act, lambda it, messages=True: None, step, softmax)

            @block.vector
            def _(dve):
                link = Link(dve, s_link)
                starts, base = [], [0]

                def make_onehot(to, group, ready):
                    dve.tensor_tensor(
                        to, wide(iota[:, :], 1, [P, ST, WINDOW]),
                        wide(dst_rel[:, bass.ds(group, SG), :].rearrange("p g k -> p (g k)"), 2, [P, ST, WINDOW]),
                        ALU.is_equal).then_inc(ready, 1)

                def before(it, messages=True):
                    if not messages:
                        return
                    if isinstance(it, tuple):
                        n = it[1]
                    else:
                        n = it * SLOTS - LAG
                    if isinstance(n, int):
                        if n + SLOTS - 1 < 3:
                            return
                        n = min(max(n - 3, 0), NS - SLOTS)
                        base[0] = n * SG
                        first = n * SG
                    else:
                        base[0] = None
                        first = (n - 3) * SG
                    starts[:] = nc.values_load_multi_w_load_instructions(
                        win[0:1, bass.ds(first, IG)], engines=DVE_ENGINE, min_val=0, max_val=N,
                        skip_runtime_bounds_check_because=CLAMPED)[1]

                def step(m, n, s):
                    q = s if m is None else (s - LAG) % SLOTS
                    q1 = (q - 1) % SLOTS
                    if exists(n, 0):
                        dve.wait_ge(loaded[q], arrived(n, q))
                        feats = en[:, q, :, 0:HID]
                        dve.tensor_tensor(feats, feats, r[:, q, :, :], ALU.mult).then_inc(multiplied, 1)
                    if m is not None:
                        if after(m, 1):
                            dve.wait_ge(turned[SG - 1], m)
                        make_onehot(onehot[:, (s + 1) % 2, :, :], (m + 1) * SG, onehot_ready)
                    if exists(n, 0):
                        dve.wait_ge(multiplied, n + 1)
                        dve.tensor_reduce(top[:, :], en[:, q, :, 0:HID].rearrange("p t (h f) -> p t h f", h=H), AX.X,
                                          ALU.max).then_inc(top_ready, 1)
                        dve.tensor_copy(weight[:, q, :],
                                        a_tab[:, bass.ds(n * SG, SG), :, :].rearrange("p g k h -> p (g k h)"))
                        dve.wait_ge(top_ready, n + 1)
                        dve.scalar_tensor_tensor(bias[:, q, :], top[:, :], -1.0,
                                                 a_tab[:, bass.ds(n * SG, SG), :, :].rearrange("p g k h -> p (g k h)"),
                                                 ALU.mult, ALU.mult).then_inc(bias_ready, 1)
                    if m is not None:
                        if after(m, 1):
                            dve.wait_ge(scored, m)
                        for g in range(SG):
                            dve.wait_ge(spread[g], m + 1)
                            dve.scalar_tensor_tensor(lrelu[:, g * K:(g + 1) * K, :], ps_e[g][:, :, 0:HID], 0.0,
                                                     wide(attn_sb[:, :], 1, [P, K, HID]), ALU.max, ALU.mult)\
                               .then_inc(masked, 1)
                            dve.tensor_copy(lin[:, g * K:(g + 1) * K, :], ps_e[g][:, :, HID:ROW])\
                               .then_inc(spread_used[g], 1)
                    if m is not None:
                        dve.wait_ge(masked, (m + 1) * SG)
                        to = e_tab[:, bass.ds(m * SG + BEFORE, SG), :, :].rearrange("p g k h -> p (g k h)")
                        dve.tensor_reduce(to, lrelu.rearrange("p t (h f) -> p (t h) f", h=H), AX.X, ALU.add)\
                           .then_inc(reduced, 1)
                    if exists(n, 1):
                        if after(n, 3):
                            dve.wait_ge(summed, n - 2)
                        make_onehot(oh_msg[:, q1 % 2, :, :], (n - 1) * SG, oh_msg_ready)
                    if m is not None:
                        dve.wait_ge(reduced, m + 1)
                        dve.wait_ge(spread_used[SG - 1], m + 1)
                        to = e_tab[:, bass.ds(m * SG + BEFORE, SG), :, :].rearrange("p g k h -> p (g k h)")
                        dve.tensor_tensor(to, to, lin[:, :, :].rearrange("p t h -> p (t h)"), ALU.add).then_inc(scored, 1)
                    if exists(n, 1):
                        dve.wait_ge(exp_done, n)
                        dve.tensor_reduce(total[:, q1, :], en[:, q1, :, 0:HID].rearrange("p t (h f) -> p t h f", h=H),
                                          AX.X, ALU.add).then_inc(sum_ready, 1)
                    if exists(n, 3):
                        dve.wait_ge(summed, n - 2)
                        for g in range(SG):
                            if after(n, 4) or g:
                                dve.wait_ge(added, (n - 3) * SG + g)
                            j = (n - 3) * SG + g - base[0] if isinstance(n, int) else (
                                s * SG + g if m is not None else (s - (NS - LAG)) % SLOTS * SG + g)
                            to = table_a[0:HID, bass.ds(starts[j], WINDOW)]
                            dve.tensor_tensor(to, to, ps_m[q1 % 2][:, g * WINDOW:(g + 1) * WINDOW], ALU.add)\
                               .then_inc(added, 1)
                    if exists(n, 1):
                        dve.wait_ge(sum_ready, n)
                        dve.reciprocal(total[:, q1, :], total[:, q1, :]).then_inc(rec_ready, 1)
                        dve.wait_ge(rec_ready, n)
                        feats = en[:, q1, :, 0:HID].rearrange("p t (h f) -> p t h f", h=H)
                        dve.tensor_tensor(feats, feats,
                                          wide(total[:, q1, :].rearrange("p (t h) -> p t h", h=H), 3, [P, ST, H, F]),
                                          ALU.mult).then_inc(msg_ready, 1)

                def arrived(n, q):
                    if not isinstance(n, int):
                        return slot_count(n, q, 16 * (1 + SG))
                    count = 0
                    for i in range(q, n + 1, SLOTS):
                        count += 16
                        for g in range(SG):
                            count += 16 * (E - (i * SG + g) * GROUP >= K)
                    return count

                def row(n, lo=0, hi=P):
                    return rowd[0:1, n, lo:hi]

                def carried(part, n, is_max, forward):
                    dve.wait_ge(ends_turned, part * 5 + 2 + n)
                    link(dve.tensor_copy(row(VALUE), ps_r[0:1, 0:P]))
                    heads = rowd[0:1, VALUE, 0:P].rearrange("a (h j) -> a h j", h=H)
                    if forward and part:
                        link(dve.tensor_copy(heads[:, :, 0], saved[:, 0 if is_max else 1, :]))
                    gate = row((NBOTH if forward else NBOTHN) if is_max else (BOTH if forward else BOTHN))
                    value, state = row(VALUE), row(STATE, 1, P + 1)
                    if not forward:
                        gate, value, state = (v[:, ::-1] for v in (gate, value, state))
                    link(dve.tensor_tensor_scan(state, gate, value, -BIG if is_max else 0.0,
                                                ALU.add if is_max else ALU.mult, ALU.max if is_max else ALU.add))
                    if forward:
                        dve.tensor_copy(saved[:, 0 if is_max else 1, :],
                                        rowd[0:1, STATE, 1:P + 1].rearrange("a (h j) -> a h j", h=H)[:, :, PART * IG])
                    came = row(STATE, 0, P) if forward else row(STATE, 2, P + 2)
                    joined = dve.tensor_tensor(cin[:, :], came, row(JOIN if forward else NEXT), ALU.mult)
                    if is_max:
                        link(joined)
                        joined = dve.tensor_tensor(cin[:, :], cin[:, :], row(NJOIN if forward else NNEXT), ALU.add)
                    joined.then_inc(cin_ready, 1)
                    dve.wait_ge(cin_turned, part * 4 + 1 + n)
                    link(dve.tensor_copy(ends[:, 3:4], ps_r[:, 256:257]))

                def totals(part, n, is_max):
                    op0, op1 = (ALU.add, ALU.max) if is_max else (ALU.mult, ALU.add)
                    gates = cneg if is_max else cont
                    start = -BIG if is_max else 0.0
                    link(dve.tensor_tensor_scan(f_row, gates[:, 0:GROUP], e_row, start, op0, op1))
                    dve.tensor_copy(ends[:, 2:3], f_row[:, GROUP - 1:GROUP]).then_inc(ends_ready, 1)
                    carried(part, n, is_max, True)
                    link(dve.tensor_tensor_scan(f_row, gates[:, 0:GROUP], e_row, ends[:, 3:4], op0, op1))
                    if not is_max:
                        link(dve.tensor_tensor(f_row, f_row, isend, ALU.mult))
                    link(dve.tensor_tensor_scan(back[:, ::-1], gates[:, 1:GROUP + 1][:, ::-1], f_row[:, ::-1],
                                                start, op0, op1))
                    dve.tensor_copy(ends[:, 2:3], back[:, 0:1]).then_inc(ends_ready, 1)
                    carried(part, n + 1, is_max, False)
                    link(dve.tensor_tensor_scan(back[:, ::-1], gates[:, 1:GROUP + 1][:, ::-1], f_row[:, ::-1],
                                                ends[:, 3:4], op0, op1))

                def softmax(part, piece):
                    if piece == 0:
                        dve.wait_ge(scored, min(IT, (part + 1) * PART) * SLOTS)
                        first = part * PART * IG
                        dve.tensor_copy(f_row.rearrange("p (k h g) -> p k h g", k=K, h=H),
                                        e_tab[:, first:first + SROWS, :, :].rearrange("p g k h -> p k h g"))\
                           .then_inc(e_staged, 1)
                        dve.wait_ge(dst_in, (part + 1) * 64)
                        dve.tensor_copy(ends[:, 0:1], dst_i[:, 0:1])
                        dve.tensor_copy(ends[:, 1:2], dst_i[:, GROUP - 1:GROUP]).then_inc(ends_ready, 1)
                        link(dve.tensor_tensor(cont[:, 1:GROUP], dst_i[:, 1:GROUP], dst_i[:, 0:GROUP - 1],
                                               ALU.is_equal))
                        dve.tensor_tensor(isend, dst_i[:, 1:GROUP + 1], dst_i[:, 0:GROUP], ALU.not_equal)\
                           .then_inc(masks_made, 1)
                        dve.wait_ge(masks_made, part + 1)
                        dve.tensor_scalar(cneg, cont, 1.0, BIG, ALU.subtract, ALU.mult)
                        dve.wait_ge(e_turned, part + 1)
                        link(dve.tensor_copy(e_row.rearrange("r (p k) -> r k p", k=K), ps_s[:, :, :]))
                        dve.wait_ge(ends_turned, part * 5 + 1)
                        link(dve.tensor_copy(rowd[0:1, FIRST:LAST + 1, 0:P],
                                             ps_r[0:1, 0:2 * P].rearrange("a (w j) -> a w j", w=2)))
                        dve.tensor_tensor(row(SAME), row(FIRST), row(LAST), ALU.is_equal)
                        link(dve.tensor_tensor(row(JOIN, 1), row(FIRST, 1), row(LAST, 0, P - 1), ALU.is_equal))
                        link(dve.memset(row(JOIN, SROWS, SROWS + 1), 0.0))
                        link(dve.tensor_copy(row(NEXT, 0, P - 1), row(JOIN, 1)))
                        dve.tensor_tensor(row(BOTH), row(SAME), row(JOIN), ALU.mult)
                        link(dve.tensor_tensor(row(BOTHN), row(SAME), row(NEXT), ALU.mult))
                        link(dve.tensor_scalar(rowd[0:1, NBOTH:NBOTHN + 1, 0:P], rowd[0:1, BOTH:BOTHN + 1, 0:P],
                                               1.0, BIG, ALU.subtract, ALU.mult))
                        link(dve.tensor_scalar(rowd[0:1, NJOIN:NNEXT + 1, 0:P], rowd[0:1, JOIN:NEXT + 1, 0:P],
                                               1.0, BIG, ALU.subtract, ALU.mult))
                    if piece == 1:
                        totals(part, 0, True)
                        dve.tensor_tensor(e_row, e_row, back, ALU.subtract).then_inc(shifted, 1)
                    if piece == 2:
                        dve.wait_ge(exped, part + 1)
                        totals(part, 2, False)
                    if piece == 3:
                        link(dve.tensor_scalar(back, back, 1e-9, None, ALU.max))
                        link(dve.reciprocal(back, back))
                        link(dve.tensor_tensor(e_row, e_row, back, ALU.mult))
                        dve.tensor_scalar(e_row, e_row, 2.0, None, ALU.min).then_inc(a_ready, 1)
                        dve.wait_ge(a_turned, part + 1)
                        lo = part * PART * IG - (SG if part else 0)
                        hi = min(G, (part + 1) * PART * IG)
                        j = lo - part * PART * IG + BEFORE
                        for h in range(H):
                            last = dve.tensor_copy(a_tab[:, lo:hi, :, h],
                                                   ps_s[:, :, h * SROWS + j:h * SROWS + j + hi - lo]
                                                   .rearrange("p k g -> p g k"))
                            last.then_inc(a_copied, 1)
                        dve.wait_ge(a_copied, (part + 1) * H)

                link(dve.memset(cont, 1.0))
                link(dve.memset(rowd[:, :, :], 0.0))
                dve.memset(saved[:, :, :], 0.0).then_inc(s_set, 1)
                make_onehot(onehot[:, 0, :, :], 0, onehot_ready)
                walk(dve, before, step, softmax)

        general_scores()
        general_softmax()
        general_sum("all_m", HID, table_a, E, messages())

        with ExitStack() as ctx:
            mean = sb("mean2", [P, NK], F32, ctx)
            var = sb("var2", [P, NK], F32, ctx)
            work = scratch[:, 0:NK * F].rearrange("p (a f) -> p a f", f=F)
            flat_rest = rest[:, :, :, :].rearrange("p c k f -> p (c k) f")
            ps = ctx.enter_context(nc.psum_tensor("ps_out", [P, NK, F], F32))
            sem = lambda n: new_sem(ctx, f"o_{n}")
            projected, link_sem, var_ready, sqrt_done, out_ready, stored = map(sem, (
                "projected", "link", "var_ready", "sqrt_done", "out_ready", "stored"))
            block = ctx.enter_context(nc.Block())

            @block.tensor
            def _(pe):
                for c in range(NCH):
                    for k in range(K):
                        m = pe.matmul(ps[:, c * K + k, :], table_a[0:HID, c * GROUP + k:(c + 1) * GROUP:K],
                                      w1_twice[:, :], start=True, stop=True)
                m.then_inc(projected, 1)

            @block.scalar
            def _(act):
                act.wait_ge(var_ready, 1)
                act.activation(var[:, :], var[:, :], ACT.Sqrt).then_inc(sqrt_done, 1)

            @block.vector
            def _(dve):
                link = Link(dve, link_sem)
                dve.wait_ge(projected, 1)
                link(dve.tensor_tensor(flat_rest, flat_rest, ps[:, :, :], ALU.add))
                layer_norm(dve, var_ready, sqrt_done, link, flat_rest, work, mean, var, flat_nodes)
                dve.memset(mean[:, 0:1], 0.0).then_inc(out_ready, 1)

            @block.sync
            def _(sp):
                sp.wait_ge(out_ready, 1)
                full = N // GROUP
                sp.dma_start(out[0:full * GROUP, :].rearrange("(c p k) f -> p c (k f)", p=P, k=K),
                             nodes[:, 0:full, :, :].rearrange("p c k f -> p c (k f)")).then_inc(stored, 16)
                left = (N - full * GROUP) // K
                sp.dma_start(out[full * GROUP:N, :].rearrange("(p k) f -> p (k f)", k=K),
                             nodes[0:left, full, :, :].rearrange("p k f -> p (k f)")).then_inc(stored, 16)
                sp.wait_ge(stored, 32)


_INS = ["x", "src", "dst", "edge_attr3_2x32", "L0_gnn_W_l_in", "L0_gnn_b_l_in", "L0_gnn_W_r_in", "L0_gnn_W_l_out",
        "L0_gnn_b_l_out", "L0_gnn_W_r_out", "L1_gnn_W1", "L1_gnn_b1", "L1_gnn_W2s", "L1_gnn_b2s", "L1_gnn_W2d",
        "L1_gnn_b2d", "L1_gnn_attn"]


def kernel(**inputs):
    import numpy as np
    import concourse.bacc as bacc
    from concourse.bass_utils import run_bass_kernel_spmd

    nc = bacc.Bacc("TRN2", target_bir_lowering=False, num_devices=1)
    arrays, args = {}, []
    for name in _INS:
        a = np.ascontiguousarray(inputs[name])
        arrays[f"in_{name}"] = a
        args.append(nc.dram_tensor(f"in_{name}", a.shape, mybir.dt.from_np(a.dtype), kind="ExternalInput").ap())
    out = nc.dram_tensor("out", arrays["in_x"].shape, F32, kind="ExternalOutput").ap()
    build(nc, *args, out)
    return run_bass_kernel_spmd(nc, [arrays], core_ids=[0]).results[0]["out"]
```
